# Optimizing a Trainium2 kernel written in Bass

```python
import numpy as np
import jax
import jax.numpy as jnp

def _softmax(x, axis=-1):
    return jax.nn.softmax(x, axis=axis)

def _gelu(x):
    return jax.nn.gelu(x, approximate=True)

def _silu(x):
    return jax.nn.silu(x)

def _sigmoid(x):
    return jax.nn.sigmoid(x)

def _layernorm(x, axis=-1, eps=1e-05):
    m = jnp.mean(x, axis=axis, keepdims=True)
    v = jnp.var(x, axis=axis, keepdims=True)
    return (x - m) / jnp.sqrt(v + eps)

def _scatter_add(tgt, idx, src, axis=0):
    return tgt.at[idx].add(src)

def _segment_sum(src, seg, n):
    return jax.ops.segment_sum(src, seg, n)
kernel_name = 'mk_rec_standalone_d1_rec_r8_1fd4c3'

def setup_inputs(seed: int=0):
    np.random.seed(seed)
    _w = jnp.asarray

    def _rec_inputs():
        import jax
        import jax.numpy as jnp
        _rk = jax.random.key(seed)
        r_candidate_features = -0.000928989 + 1.00043 * jax.random.normal(jax.random.fold_in(_rk, 1), (512, 128), jnp.float32)
        r_history_features = -7.74141e-05 + 0.99993 * jax.random.normal(jax.random.fold_in(_rk, 2), (512, 200, 128), jnp.float32)
        r_history_length = jax.random.randint(jax.random.fold_in(_rk, 3), (512,), 1, 201, jnp.int32)
        return (r_candidate_features, r_history_features, r_history_length)
    r_candidate_features, r_history_features, r_history_length = _rec_inputs()

    def _L0_rec_setup():
        import jax, jax.numpy as jnp
        import numpy as np
        B, S, F, E, A = (1024, 200, 128, 64, 64)
        H1, H2, H3 = (128, 64, 32)
        EPS = 1e-05

        def _bn(x, g, be, m, v):
            return (x - m) * jax.lax.rsqrt(v + EPS) * g + be
        key = jax.random.key(seed)
        ks = jax.random.split(key, 24)
        w = lambda k, shape: jax.random.normal(k, shape, dtype=jnp.float32) * 0.05
        inp = {'candidate_features': jax.random.normal(ks[0], (B, F), dtype=jnp.float32), 'history_features': jax.random.normal(ks[1], (B, S, F), dtype=jnp.float32), 'history_length': jax.random.randint(ks[2], (B,), 1, S + 1, dtype=jnp.int32), 'Wi': w(ks[3], (F, E)), 'bi': jnp.zeros((E,), jnp.float32), 'Wq': w(ks[4], (E, A)), 'Wk': w(ks[5], (E, A)), 'Wv': w(ks[6], (A,)), 'W1': w(ks[7], (3 * E, H1)), 'b1': jnp.zeros((H1,), jnp.float32), 'g1': jnp.ones((H1,), jnp.float32), 'be1': jnp.zeros((H1,), jnp.float32), 'm1': w(ks[8], (H1,)), 'v1': jax.random.uniform(ks[9], (H1,), jnp.float32, 0.5, 1.5), 'W2': w(ks[10], (H1, H2)), 'b2': jnp.zeros((H2,), jnp.float32), 'g2': jnp.ones((H2,), jnp.float32), 'be2': jnp.zeros((H2,), jnp.float32), 'm2': w(ks[11], (H2,)), 'v2': jax.random.uniform(ks[12], (H2,), jnp.float32, 0.5, 1.5), 'W3': w(ks[13], (H2, H3)), 'b3': jnp.zeros((H3,), jnp.float32), 'g3': jnp.ones((H3,), jnp.float32), 'be3': jnp.zeros((H3,), jnp.float32), 'm3': w(ks[14], (H3,)), 'v3': jax.random.uniform(ks[15], (H3,), jnp.float32, 0.5, 1.5), 'Wo': w(ks[16], (H3, 1)), 'bo': jnp.zeros((1,), jnp.float32)}
        return inp
    _L0_rec_all = _L0_rec_setup()
    _L0_rec_in = {k: v for k, v in _L0_rec_all.items() if k in ('Wi', 'bi', 'Wq', 'Wk', 'Wv', 'W1', 'b1', 'g1', 'be1', 'm1', 'v1', 'W2', 'b2', 'g2', 'be2', 'm2', 'v2', 'W3', 'b3', 'g3', 'be3', 'm3', 'v3', 'Wo', 'bo')}
    del _L0_rec_all
    return {'r_candidate_features': r_candidate_features, 'r_history_features': r_history_features, 'r_history_length': r_history_length, 'L0_rec_Wi': _L0_rec_in['Wi'], 'L0_rec_bi': _L0_rec_in['bi'], 'L0_rec_Wq': _L0_rec_in['Wq'], 'L0_rec_Wk': _L0_rec_in['Wk'], 'L0_rec_Wv': _L0_rec_in['Wv'], 'L0_rec_W1': _L0_rec_in['W1'], 'L0_rec_b1': _L0_rec_in['b1'], 'L0_rec_g1': _L0_rec_in['g1'], 'L0_rec_be1': _L0_rec_in['be1'], 'L0_rec_m1': _L0_rec_in['m1'], 'L0_rec_v1': _L0_rec_in['v1'], 'L0_rec_W2': _L0_rec_in['W2'], 'L0_rec_b2': _L0_rec_in['b2'], 'L0_rec_g2': _L0_rec_in['g2'], 'L0_rec_be2': _L0_rec_in['be2'], 'L0_rec_m2': _L0_rec_in['m2'], 'L0_rec_v2': _L0_rec_in['v2'], 'L0_rec_W3': _L0_rec_in['W3'], 'L0_rec_b3': _L0_rec_in['b3'], 'L0_rec_g3': _L0_rec_in['g3'], 'L0_rec_be3': _L0_rec_in['be3'], 'L0_rec_m3': _L0_rec_in['m3'], 'L0_rec_v3': _L0_rec_in['v3'], 'L0_rec_Wo': _L0_rec_in['Wo'], 'L0_rec_bo': _L0_rec_in['bo']}

def reference(r_candidate_features, r_history_features, r_history_length, L0_rec_Wi, L0_rec_bi, L0_rec_Wq, L0_rec_Wk, L0_rec_Wv, L0_rec_W1, L0_rec_b1, L0_rec_g1, L0_rec_be1, L0_rec_m1, L0_rec_v1, L0_rec_W2, L0_rec_b2, L0_rec_g2, L0_rec_be2, L0_rec_m2, L0_rec_v2, L0_rec_W3, L0_rec_b3, L0_rec_g3, L0_rec_be3, L0_rec_m3, L0_rec_v3, L0_rec_Wo, L0_rec_bo):
    import jax
    import jax.numpy as jnp

    def _L0_rec_ref(candidate_features, history_features, history_length, Wi, bi, Wq, Wk, Wv, W1, b1, g1, be1, m1, v1, W2, b2, g2, be2, m2, v2, W3, b3, g3, be3, m3, v3, Wo, bo):
        import jax, jax.numpy as jnp
        import numpy as np
        B, S, F, E, A = (1024, 200, 128, 64, 64)
        H1, H2, H3 = (128, 64, 32)
        EPS = 1e-05

        def _bn(x, g, be, m, v):
            return (x - m) * jax.lax.rsqrt(v + EPS) * g + be
        cand = candidate_features @ Wi + bi
        hist = history_features @ Wi + bi
        qh = cand @ Wq
        kh = hist @ Wk
        hidden = jax.nn.relu(qh[:, None, :] + kh)
        scores = hidden @ Wv
        seq = jnp.arange(hist.shape[1])
        mask = seq[None, :] < history_length[:, None]
        scores = jnp.where(mask, scores, -1000000000.0)
        attn = jax.nn.softmax(scores, axis=1)
        interest = jnp.einsum('bs,bse->be', attn, hist)
        lens = history_length[:, None].astype(hist.dtype)
        avg = jnp.sum(hist * mask[:, :, None], axis=1) / lens
        x = jnp.concatenate([interest, cand, avg], axis=1)
        x = jax.nn.relu(_bn(x @ W1 + b1, g1, be1, m1, v1))
        x = jax.nn.relu(_bn(x @ W2 + b2, g2, be2, m2, v2))
        x = jax.nn.relu(_bn(x @ W3 + b3, g3, be3, m3, v3))
        logits = x @ Wo + bo
        return jax.nn.sigmoid(logits)[:, 0]
    y = _L0_rec_ref(r_candidate_features, r_history_features, r_history_length, L0_rec_Wi, L0_rec_bi, L0_rec_Wq, L0_rec_Wk, L0_rec_Wv, L0_rec_W1, L0_rec_b1, L0_rec_g1, L0_rec_be1, L0_rec_m1, L0_rec_v1, L0_rec_W2, L0_rec_b2, L0_rec_g2, L0_rec_be2, L0_rec_m2, L0_rec_v2, L0_rec_W3, L0_rec_b3, L0_rec_g3, L0_rec_be3, L0_rec_m3, L0_rec_v3, L0_rec_Wo, L0_rec_bo)
    return y

_drawn_inputs = setup_inputs


def setup_inputs(seed=0):
    import zlib

    import numpy as np

    out = dict(_drawn_inputs(seed))
    spreads = {'L0_rec_bi': (0.0, 0.8),
     'L0_rec_b1': (0.0, 2.0),
     'L0_rec_g1': (1.0, 0.6),
     'L0_rec_be1': (0.0, 0.8),
     'L0_rec_b2': (0.0, 2.0),
     'L0_rec_g2': (1.0, 0.6),
     'L0_rec_be2': (0.0, 2.0),
     'L0_rec_b3': (0.0, 2.0),
     'L0_rec_g3': (1.0, 0.6),
     'L0_rec_be3': (0.0, 2.0)}
    factors = {'r_candidate_features': 8.0,
     'r_history_features': 8.0,
     'L0_rec_Wi': 8.0,
     'L0_rec_Wq': 8.0,
     'L0_rec_Wk': 8.0,
     'L0_rec_Wv': 8.0,
     'L0_rec_W1': 8.0,
     'L0_rec_m1': 37.767,
     'L0_rec_v1': 8.0,
     'L0_rec_W2': 8.0,
     'L0_rec_m2': 64.0,
     'L0_rec_v2': 8.0,
     'L0_rec_W3': 8.0,
     'L0_rec_m3': 64.0,
     'L0_rec_v3': 8.0,
     'L0_rec_Wo': 3.724}
    for name, (base, spread) in spreads.items():
        noise = np.random.default_rng([zlib.crc32(name.encode()), seed]).standard_normal(out[name].shape)
        drawn = base * np.exp(spread * noise) if base else spread * noise
        out[name] = jnp.asarray(drawn.astype(out[name].dtype))
    for name, factor in factors.items():
        out[name] = (out[name] * factor).astype(out[name].dtype)
    return out
```

```python
from contextlib import ExitStack

import concourse.bass as bass
from concourse import mybir

F32 = mybir.dt.float32
BF16 = mybir.dt.bfloat16
I32 = mybir.dt.int32
ALU = mybir.AluOpType
ACT = mybir.ActivationFunctionType
AX_X = mybir.AxisListType.X

USERS, SEQ, FEAT, EMB = 512, 200, 128, 64
HID1, HID2, HID3 = 128, 64, 32
BN_EPS = 1e-05
MASKED = -1000000000.0

HALF = USERS // 2
QUADS = HALF // 2
QCOLS = 2 * SEQ
BATCHES = HALF // 4
SB_PAIRS = 16
SB_QUADS = SB_PAIRS // 2
SB_BATCHES = SB_PAIRS // 4
SUPERBLOCKS = HALF // SB_PAIRS
BODY_QUADS = 2 * SB_QUADS
BODY_PAIRS = 2 * SB_PAIRS
BODIES = QUADS // BODY_QUADS
HID_SLOTS = 4
DELAY = 13
COPIES = 3
USER_ROWS = 8

PARAM_COLS = {}
_at = 0
for _name, _width in (("wi", EMB), ("wiT", FEAT), ("wk", EMB), ("wq", EMB), ("bi", 1), ("wv", 1),
                      ("keep1", 1), ("keep2", 1), ("w1", 3 * HID1), ("w2", HID2), ("w3", HID3), ("wo", 1),
                      ("bo", 1), ("b", 3), ("g", 3), ("be", 3), ("m", 3), ("v", 3)):
    PARAM_COLS[_name] = (_at, _width)
    _at += _width
PARAMS = _at
EARLY = PARAM_COLS["w1"][0]


def build(nc, hist_dram, cand_dram, params_dram, lens_dram, out_dram):
    with ExitStack() as ctx:
        def sb(name, shape, dt=F32):
            return ctx.enter_context(nc.sbuf_tensor(name, shape, dt))

        def psum(name, shape):
            return ctx.enter_context(nc.psum_tensor(name, shape, F32))

        def sem(name):
            return ctx.enter_context(nc.semaphore(name))

        params = sb("params", [128, PARAMS])

        def param(name, rows=slice(0, 128)):
            at, width = PARAM_COLS[name]
            return params[rows, at:at + width]

        history = sb("history", [128, SB_BATCHES, 2, 4, SEQ])
        candT = sb("candT", [128, USERS])
        lens_raw = sb("lens_raw", [128, HALF + SUPERBLOCKS], I32)
        lens = sb("lens", [128, HALF + SUPERBLOCKS])
        pair_len = lens[:, 0:HALF]
        row_len = lens[:, HALF:HALF + SUPERBLOCKS]
        wik = sb("wik", [128, EMB])
        wv_rows = sb("wv_rows", [128, SB_BATCHES, 32])
        cand = sb("cand", [128, HALF])
        query = sb("query", [128, HALF])
        query_now = sb("query_now", [128, BODY_PAIRS])
        len_now = sb("len_now", [128, BODY_PAIRS])
        rowlen_now = sb("rowlen_now", [128, 2])
        item = sb("item", [128, SEQ])
        spread = sb("spread", [128, SB_PAIRS, 2, EMB], BF16)
        hidden = sb("hidden", [128, HID_SLOTS, QCOLS])
        kept = sb("kept", [128, BODY_QUADS, 2, SEQ])
        scratch = sb("scratch", [128, 2, SEQ])
        valid = sb("valid", [128, SEQ], I32)
        scores = sb("scores", [128, SEQ])
        neg_max = sb("neg_max", [128, 1])
        weights = sb("weights", [128, SEQ])
        weight_sum = sb("weight_sum", [128, 1])
        inv_sum = sb("inv_sum", [128, 1])
        part_a = sb("part_a", [128, SEQ], BF16)
        part_b = sb("part_b", [128, SEQ], BF16)
        attn = sb("attn", [128, SEQ])
        rest = sb("rest", [128, SEQ])
        parts = sb("parts", [128, 2, SEQ], BF16)
        sum_now = sb("sum_now", [128, BODY_PAIRS])
        interest_now = sb("interest_now", [128, BODY_PAIRS])
        hist_sum = sb("hist_sum", [128, HALF])
        interest = sb("interest", [128, HALF])
        average = sb("average", [128, HALF])
        inv_len = sb("inv_len", [128, HALF])
        count = sb("count", [128, HALF])
        bn_scale = sb("bn_scale", [128, 3])
        bn_shift = sb("bn_shift", [128, 3])
        bn_power = sb("bn_power", [128, 3])
        x1 = sb("x1", [HID1, USERS])
        x2 = sb("x2", [HID2, USERS])
        x3 = sb("x3", [HID3, USERS])
        result = sb("result", [1, USERS])

        key_ps = psum("key_ps", [128, 2, 512])
        hist_ps = psum("hist_ps", [128, 2, 512])
        score_ps = psum("score_ps", [128, 2, 512])
        attn_ps = psum("attn_ps", [128, 2, 512])

        early_landed = sem("early_landed")
        late_landed = sem("late_landed")
        cand_landed = sem("cand_landed")
        lens_landed = sem("lens_landed")
        batch_landed = [sem(f"batch_landed{i}") for i in range(SB_BATCHES)]
        item_made = sem("item_made")
        spread_made = sem("spread_made")
        wv_steps = sem("wv_steps")
        wv_ready = sem("wv_ready")
        lens_ready = sem("lens_ready")
        wik_product = sem("wik_product")
        wik_ready = sem("wik_ready")
        cand_product = sem("cand_product")
        cand_ready = sem("cand_ready")
        query_product = sem("query_product")
        query_ready = sem("query_ready")
        query_staged = sem("query_staged")
        len_staged = sem("len_staged")
        rowlen_staged = sem("rowlen_staged")
        key_ready = sem("key_ready")
        hist_ready = sem("hist_ready")
        relu_done = sem("relu_done")
        masked_summed = sem("masked_summed")
        batch_scored = sem("batch_scored")
        mask_ready = sem("mask_ready")
        scores_taken = sem("scores_taken")
        max_ready = sem("max_ready")
        exp_done = sem("exp_done")
        inv_ready = sem("inv_ready")
        split_steps = sem("split_steps")
        parts_ready = sem("parts_ready")
        attn_spread = sem("attn_spread")
        attn_summed = sem("attn_summed")
        sums_stored = sem("sums_stored")
        bn_steps = sem("bn_steps")
        bn_ready = sem("bn_ready")
        mean_steps = sem("mean_steps")
        features_ready = sem("features_ready")
        z1_ready = sem("z1_ready")
        x1_ready = sem("x1_ready")
        z2_ready = sem("z2_ready")
        x2_ready = sem("x2_ready")
        z3_ready = sem("z3_ready")
        x3_ready = sem("x3_ready")
        z4_ready = sem("z4_ready")
        result_ready = sem("result_ready")
        result_stored = sem("result_stored")

        block = ctx.enter_context(nc.Block())

        def wait(eng, semaphore, value):
            if not isinstance(value, int) or value > 0:
                eng.wait_ge(semaphore, value)

        def wait_apart(eng, *waits):
            waits = [(s, v if isinstance(v, int) else eng.to_reg(v)) for s, v in waits]
            eng.wait_ge(lens_ready, 1)
            for semaphore, value in waits:
                wait(eng, semaphore, value)

        @block.sync
        def _(sp):
            def load(t, parity, slot):
                if isinstance(t, int) and t == 0 and parity == 0:
                    pass
                else:
                    wait(sp, hist_ready, BODY_QUADS * t + SB_QUADS * (parity - 1) + 2 * slot + 2)
                n = SB_BATCHES * (2 * t + parity) + slot
                sp.dma_start(history[:, slot, :, :, :].rearrange("f h p s -> f (h p s)"),
                             hist_dram[bass.ds(n, 1), :, :].rearrange("a f c -> (a f) c")).then_inc(batch_landed[slot], 16)

            def body(t):
                for parity in range(2):
                    for slot in range(SB_BATCHES):
                        load(t, parity, slot)

            body(0)
            with sp.Fori(1, BODIES) as t:
                body(t)
            sp.wait_ge(result_ready, 1)
            sp.dma_start(out_dram.rearrange("(a n) -> a n", a=1), result[:, :]).then_inc(result_stored, 16)
            sp.wait_ge(result_stored, 16)

        @block.gpsimd
        def _(pool):
            pool.iota(item[:, :], pattern=[[1, SEQ]], base=0, channel_multiplier=0,
                      allow_small_or_imprecise_dtypes=True).then_inc(item_made, 1)
            pool.memset(wv_rows[:, :, :], 0.0).then_inc(wv_steps, 1)
            pool.wait_ge(wv_steps, 1)
            wv_view = wv_rows[:, :, :].rearrange("p k (c u) -> p k c u", u=USER_ROWS)
            for h in range(2):
                v = wv_view[64 * h:64 * h + 64, :, 0:COPIES, :]
                pool.affine_select(out=v, in_=v, compare_op=ALU.not_equal, fill=1.0, base=h,
                                   pattern=[[2, SB_BATCHES], [0, COPIES], [-1, USER_ROWS]],
                                   channel_multiplier=0).then_inc(wv_steps, 1)
            pool.wait_ge(wv_steps, 3)
            pool.wait_ge(early_landed, 16)
            pool.tensor_scalar(wv_rows[:, :, :], wv_rows[:, :, :], param("wv"), None, ALU.mult).then_inc(wv_ready, 1)

            flat = spread[:, :, :, :].rearrange("p (k q) h e -> p k q (h e)", q=4)
            pool.memset(spread[:, :, :, :], 0.0).then_inc(spread_made, 1)
            for copy in range(COPIES):
                for h in range(2):
                    v = flat[:, :, :, EMB * h:EMB * h + EMB]
                    if h == 0:
                        pool.wait_ge(spread_made, 2 * copy + 1)
                    pool.affine_select(out=v, in_=v, compare_op=ALU.not_equal, fill=1.0,
                                       base=-USER_ROWS * copy - h, pattern=[[-2, SB_BATCHES], [-32, 4], [0, EMB]],
                                       channel_multiplier=1).then_inc(spread_made, 1)

            pool.wait_ge(lens_ready, 1)

            def prepare(t, parity, first):
                if not first:
                    wait_apart(pool, (exp_done, 2 * t + parity))
                if parity == 0:
                    wait(pool, mask_ready, 4 * t)
                    pool.tensor_copy(rowlen_now[:, :], row_len[:, bass.ds(2 * t, 2)]).then_inc(rowlen_staged, 1)
                pool.memset(scores[:, :], MASKED).then_inc(mask_ready, 1)
                wait_apart(pool, (rowlen_staged, t + 1))
                pool.tensor_scalar(valid[:, :], item[:, :], rowlen_now[:, parity:parity + 1], None,
                                   ALU.is_lt).then_inc(mask_ready, 1)

            def split(t, parity):
                done = 4 * (2 * t + parity)
                wait_apart(pool, (exp_done, 2 * t + parity + 1), (inv_ready, 2 * t + parity + 1),
                           (parts_ready, 2 * t + parity))
                pool.tensor_scalar(attn[:, :], weights[:, :], inv_sum[:, 0:1], None, ALU.mult).then_inc(split_steps, 1)
                pool.tensor_scalar(part_a[:, :], weights[:, :], inv_sum[:, 0:1], param("keep1"),
                                   ALU.mult, ALU.mult).then_inc(split_steps, 1)
                wait(pool, split_steps, done + 2)
                pool.tensor_tensor(rest[:, :], attn[:, :], part_a[:, :], ALU.subtract).then_inc(split_steps, 1)
                wait_apart(pool, (split_steps, done + 3))
                pool.tensor_scalar(part_b[:, :], rest[:, :], param("keep2"), None, ALU.mult).then_inc(split_steps, 1)
                wait(pool, split_steps, done + 4)
                wait(pool, attn_spread, SB_QUADS * (2 * t + parity - 1))
                pool.tensor_tensor(parts[:, parity, :], rest[:, :], part_b[:, :],
                                   ALU.subtract).then_inc(parts_ready, 1)

            def body(t, last=False):
                for parity in range(2):
                    split(t, parity)
                    if parity == 0:
                        prepare(t, 1, False)
                    elif not last:
                        prepare(t + 1, 0, False)

            prepare(0, 0, True)
            pool.wait_ge(late_landed, 16)
            pool.memset(bn_power[:, :], -0.5).then_inc(bn_steps, 1)
            pool.tensor_scalar(bn_scale[:, :], param("v"), BN_EPS, None, ALU.add).then_inc(bn_steps, 1)
            pool.tensor_tensor(bn_shift[:, :], param("b"), param("m"), ALU.subtract).then_inc(bn_steps, 1)
            pool.wait_ge(bn_steps, 3)
            pool.tensor_tensor(bn_scale[:, :], bn_scale[:, :], bn_power[:, :], ALU.pow).then_inc(bn_steps, 1)
            pool.wait_ge(bn_steps, 4)
            pool.tensor_tensor(bn_scale[:, :], bn_scale[:, :], param("g"), ALU.mult).then_inc(bn_steps, 1)
            pool.wait_ge(bn_steps, 5)
            pool.tensor_tensor(bn_shift[:, :], bn_shift[:, :], bn_scale[:, :], ALU.mult).then_inc(bn_steps, 1)
            pool.wait_ge(bn_steps, 6)
            pool.tensor_tensor(bn_shift[:, :], bn_shift[:, :], param("be"), ALU.add).then_inc(bn_ready, 1)
            body(0)
            with pool.Fori(1, BODIES - 1) as t:
                body(t)
            body(BODIES - 1, True)

        @block.scalar
        def _(act):
            act.dma_start(params[:, 0:EARLY], params_dram[:, 0:EARLY]).then_inc(early_landed, 16)
            act.dma_start(candT[:, :], cand_dram).then_inc(cand_landed, 16)
            act.dma_start(lens_raw[:, :], lens_dram).then_inc(lens_landed, 16)
            act.dma_start(params[:, EARLY:PARAMS], params_dram[:, EARLY:PARAMS]).then_inc(late_landed, 16)

            def relu_quad(t, r):
                g = BODY_QUADS * t + r
                wait(act, key_ready, g + 1)
                if not (isinstance(g, int) and g < HID_SLOTS):
                    wait(act, batch_scored, 8 * t + (r - HID_SLOTS) // 2 + 1)
                for u in range(2):
                    act.activation(hidden[:, r % HID_SLOTS, u * SEQ:(u + 1) * SEQ],
                                   key_ps[:, r % 2, u * SEQ:(u + 1) * SEQ], ACT.Relu,
                                   bias=query_now[:, 2 * r + u:2 * r + u + 1]).then_inc(relu_done, 1)

            def exponent(s):
                wait(act, max_ready, s + 1)
                wait(act, split_steps, 4 * s)
                act.activation(weights[:, :], scores[:, :], ACT.Exp, bias=neg_max[:, 0:1],
                               accum_out=weight_sum[:, 0:1]).then_inc(exp_done, 1)

            def body(t):
                wait(act, relu_done, BODY_PAIRS * t)
                act.activation(query_now[:, :], query[:, bass.ds(BODY_PAIRS * t, BODY_PAIRS)],
                               ACT.Copy).then_inc(query_staged, 1)
                wait(act, query_staged, t + 1)
                for r in range(BODY_QUADS):
                    relu_quad(t, r)
                    if r == 9:
                        exponent(2 * t)
                    if r == 1 and not (isinstance(t, int) and t == 0):
                        exponent(2 * t - 1)

            act.wait_ge(query_ready, 2)
            body(0)
            with act.Fori(1, BODIES) as t:
                body(t)
            exponent(SUPERBLOCKS - 1)

            act.wait_ge(bn_ready, 1)
            act.wait_ge(z1_ready, 1)
            for h in range(2):
                act.activation(x1[:, h * HALF:(h + 1) * HALF], key_ps[:, h, 0:HALF], ACT.Relu,
                               bias=bn_shift[:, 0:1], scale=bn_scale[:, 0:1]).then_inc(x1_ready, 1)
            act.wait_ge(z2_ready, 1)
            act.activation(x2[:, :], hist_ps[0:HID2, 0, :], ACT.Relu, bias=bn_shift[0:HID2, 1:2],
                           scale=bn_scale[0:HID2, 1:2]).then_inc(x2_ready, 1)
            act.wait_ge(z3_ready, 1)
            act.activation(x3[:, :], hist_ps[0:HID3, 1, :], ACT.Relu, bias=bn_shift[0:HID3, 2:3],
                           scale=bn_scale[0:HID3, 2:3]).then_inc(x3_ready, 1)
            act.wait_ge(z4_ready, 1)
            act.activation(result[:, :], score_ps[0:1, 0, :], ACT.Sigmoid,
                           bias=param("bo", slice(0, 1))).then_inc(result_ready, 1)

        @block.tensor
        def _(pe):
            pe.wait_ge(early_landed, 16)
            pe.matmul(attn_ps[:, 0, 0:EMB], param("wiT", slice(0, EMB)), param("wk", slice(0, EMB)),
                      start=True, stop=True).then_inc(wik_product, 1)
            pe.wait_ge(cand_landed, 16)
            for h in range(2):
                pe.matmul(attn_ps[64 * h:64 * h + 64, 1, 0:HALF], param("wi"), candT[:, h * HALF:(h + 1) * HALF],
                          start=True, stop=True).then_inc(cand_product, 1)
            pe.wait_ge(cand_ready, 1)
            for h in range(2):
                rows = slice(64 * h, 64 * h + 64)
                pe.matmul(score_ps[rows, h, 0:HALF], param("wq", rows), cand[rows, :], start=True, stop=False)
                pe.matmul(score_ps[rows, h, 0:HALF], param("wk", rows),
                          param("bi", rows).broadcast_to([64, HALF]), start=False, stop=True).then_inc(query_product, 1)
            pe.wait_ge(wik_ready, 1)

            def project(t, r):
                g = BODY_QUADS * t + r
                slot, pair = (r % SB_QUADS) // 2, 2 * (r % 2)
                if r % 2 == 0:
                    wait(pe, batch_landed[slot], 16 * (2 * t + r // SB_QUADS + 1))
                items = [history[:, slot, h, pair:pair + 2, :].rearrange("f p s -> f (p s)") for h in range(2)]
                wait(pe, relu_done, 2 * (g - 2) + 2)
                pe.matmul(key_ps[0:64, r % 2, 0:QCOLS], wik[:, :], items[0], start=True, stop=True)
                pe.matmul(key_ps[64:128, r % 2, 0:QCOLS], wik[:, :], items[1], start=True, stop=True).then_inc(key_ready, 1)
                wait(pe, masked_summed, 2 * (g - 2) + 2)
                pe.matmul(hist_ps[0:64, r % 2, 0:QCOLS], param("wi"), items[0], start=True, stop=True)
                pe.matmul(hist_ps[64:128, r % 2, 0:QCOLS], param("wi"), items[1], start=True, stop=True).then_inc(hist_ready, 1)

            def score(t, r):
                first_quad = (r - 2) % BODY_QUADS
                k = first_quad // 2 % SB_BATCHES
                bank = first_quad // SB_QUADS
                superblock = 2 * t + (r - 2) // SB_QUADS
                wait(pe, relu_done, 2 * (BODY_QUADS * t + r))
                if k == 0:
                    wait(pe, scores_taken, superblock - 1)
                for q in range(4):
                    quad = first_quad + q // 2
                    product = pe.matmul(score_ps[32 * q:32 * q + 32, bank, 0:SEQ], wv_rows[:, k, :],
                                        hidden[:, quad % HID_SLOTS, (q % 2) * SEQ:(q % 2 + 1) * SEQ],
                                        start=(k == 0), stop=(k == SB_BATCHES - 1))
                product.then_inc(batch_scored, 1)

            def spread_attn(t, r):
                at = r - DELAY
                quad = at % BODY_QUADS
                if quad % SB_QUADS == 0:
                    wait(pe, parts_ready, 2 * t + at // SB_QUADS + 1)
                wait(pe, attn_summed, 2 * (BODY_QUADS * t + at - 2) + 2)
                for u in range(2):
                    pair = 2 * (quad % SB_QUADS) + u
                    product = pe.matmul(attn_ps[:, quad % 2, u * SEQ:(u + 1) * SEQ],
                                        spread[:, pair, :, :].rearrange("p h e -> p (h e)"),
                                        parts[:, quad // SB_QUADS, :], start=True, stop=True)
                product.then_inc(attn_spread, 1)

            def body(t):
                for r in range(BODY_QUADS):
                    started = not isinstance(t, int) or BODY_QUADS * t + r >= 2
                    project(t, r)
                    if r % 2 == 0 and started:
                        score(t, r)
                    if not isinstance(t, int) or BODY_QUADS * t + r >= DELAY:
                        spread_attn(t, r)

            pe.wait_ge(query_ready, 2)
            pe.wait_ge(wv_ready, 1)
            pe.wait_ge(spread_made, 1 + 2 * COPIES)
            body(0)
            with pe.Fori(1, BODIES) as t:
                body(t)
            score(BODIES, 0)
            for r in range(DELAY):
                spread_attn(BODIES, r)

            pe.wait_ge(late_landed, 16)
            pe.wait_ge(features_ready, 1)
            w1 = param("w1").rearrange("p (c n) -> p c n", c=3)
            for h in range(2):
                rows = slice(64 * h, 64 * h + 64)
                for c, x in enumerate((interest, cand, average)):
                    product = pe.matmul(key_ps[:, h, 0:HALF], w1[rows, c, :], x[rows, :], start=(c == 0), stop=(c == 2))
            product.then_inc(z1_ready, 1)
            pe.wait_ge(x1_ready, 2)
            pe.matmul(hist_ps[0:HID2, 0, :], param("w2"), x1[:, :], start=True, stop=True).then_inc(z2_ready, 1)
            pe.wait_ge(x2_ready, 1)
            pe.matmul(hist_ps[0:HID3, 1, :], param("w3", slice(0, HID2)), x2[:, :], start=True, stop=True).then_inc(z3_ready, 1)
            pe.wait_ge(x3_ready, 1)
            pe.matmul(score_ps[0:1, 0, :], param("wo", slice(0, HID3)), x3[:, :], start=True, stop=True).then_inc(z4_ready, 1)

        @block.vector
        def _(dve):
            dve.wait_ge(wik_product, 1)
            dve.tensor_copy(wik[:, :], attn_ps[:, 0, 0:EMB]).then_inc(wik_ready, 1)
            dve.wait_ge(early_landed, 16)
            dve.wait_ge(cand_product, 2)
            dve.tensor_scalar(cand[:, :], attn_ps[:, 1, 0:HALF], param("bi"), None, ALU.add).then_inc(cand_ready, 1)
            dve.wait_ge(lens_landed, 16)
            dve.tensor_copy(lens[:, :], lens_raw[:, :]).then_inc(lens_ready, 1)
            dve.wait_ge(query_product, 2)
            for h in range(2):
                rows = slice(64 * h, 64 * h + 64)
                dve.tensor_copy(query[rows, :], score_ps[rows, h, 0:HALF]).then_inc(query_ready, 1)
            dve.wait_ge(item_made, 1)
            dve.wait_ge(lens_ready, 1)

            def masked_sum(t, r):
                wait(dve, hist_ready, BODY_QUADS * t + r + 1)
                for u in range(2):
                    col = 2 * r + u
                    dve.scalar_tensor_tensor(out=kept[:, r, u, :], in0=item[:, :], scalar=len_now[:, col:col + 1],
                                             in1=hist_ps[:, r % 2, u * SEQ:(u + 1) * SEQ], op0=ALU.is_lt, op1=ALU.mult,
                                             accum_out=sum_now[:, col:col + 1]).then_inc(masked_summed, 1)

            def attended_sum(t, r):
                at = r - DELAY
                quad = at % BODY_QUADS
                wait(dve, attn_spread, BODY_QUADS * t + at + 1)
                wait(dve, attn_summed, 2 * (BODY_QUADS * t + at))
                for u in range(2):
                    col = 2 * quad + u
                    dve.tensor_tensor_reduce(scratch[:, u, :], attn_ps[:, quad % 2, u * SEQ:(u + 1) * SEQ],
                                             kept[:, quad, u, :], 1.0, 0.0, ALU.mult, ALU.add,
                                             interest_now[:, col:col + 1]).then_inc(attn_summed, 1)

            def maximum(s, bank):
                wait_apart(dve, (batch_scored, SB_BATCHES * (s + 1)), (mask_ready, 2 * (s + 1)))
                dve.copy_predicated(scores[:, :], valid[:, :], score_ps[:, bank, 0:SEQ]).then_inc(scores_taken, 1)
                wait(dve, scores_taken, s + 1)
                dve.reduce_max(neg_max[:, 0:1], scores[:, :], AX_X, negate=True).then_inc(max_ready, 1)

            def invert(s):
                wait(dve, exp_done, s + 1)
                dve.reciprocal(inv_sum[:, 0:1], weight_sum[:, 0:1]).then_inc(inv_ready, 1)

            def store_interest(t):
                wait(dve, attn_summed, BODY_PAIRS * (t + 1))
                dve.tensor_copy(interest[:, bass.ds(BODY_PAIRS * t, BODY_PAIRS)], interest_now[:, :]).then_inc(sums_stored, 1)

            def body(t):
                started = not (isinstance(t, int) and t == 0)
                wait(dve, sums_stored, 2 * t - 1)
                dve.tensor_copy(len_now[:, :], pair_len[:, bass.ds(BODY_PAIRS * t, BODY_PAIRS)]).then_inc(len_staged, 1)
                wait(dve, len_staged, t + 1)
                for r in range(BODY_QUADS):
                    if r == 9:
                        maximum(2 * t, 0)
                    if r == 10:
                        invert(2 * t)
                    if r == 1 and started:
                        maximum(2 * t - 1, 1)
                    if r == 2 and started:
                        invert(2 * t - 1)
                    masked_sum(t, r)
                    if started and r == DELAY:
                        wait(dve, sums_stored, 2 * t)
                    if started or r >= DELAY:
                        attended_sum(t, r)
                    if started and r == DELAY - 1:
                        store_interest(t - 1)
                wait(dve, masked_summed, BODY_PAIRS * (t + 1))
                dve.tensor_copy(hist_sum[:, bass.ds(BODY_PAIRS * t, BODY_PAIRS)], sum_now[:, :]).then_inc(sums_stored, 1)

            body(0)
            with dve.Fori(1, BODIES) as t:
                body(t)
            maximum(SUPERBLOCKS - 1, 1)
            invert(SUPERBLOCKS - 1)

            dve.reciprocal(inv_len[:, :], pair_len).then_inc(mean_steps, 1)
            dve.tensor_scalar(count[:, :], pair_len, float(SEQ), 0.0, ALU.min, ALU.max).then_inc(mean_steps, 1)
            dve.wait_ge(mean_steps, 2)
            dve.wait_ge(sums_stored, 2 * BODIES - 1)
            dve.scalar_tensor_tensor(out=average[:, :], in0=count[:, :], scalar=param("bi"), in1=hist_sum[:, :],
                                     op0=ALU.mult, op1=ALU.add).then_inc(mean_steps, 1)
            dve.wait_ge(mean_steps, 3)
            dve.tensor_tensor(average[:, :], average[:, :], inv_len[:, :], ALU.mult).then_inc(mean_steps, 1)
            for r in range(DELAY):
                attended_sum(BODIES, r)
            store_interest(BODIES - 1)
            dve.wait_ge(sums_stored, 2 * BODIES)
            dve.wait_ge(mean_steps, 4)
            dve.tensor_scalar(interest[:, :], interest[:, :], param("bi"), None, ALU.add).then_inc(features_ready, 1)


def kernel(**inputs):
    import numpy as np
    import concourse.bacc as bacc
    from concourse.bass_utils import run_bass_kernel_spmd

    take = {name: np.ascontiguousarray(value) for name, value in inputs.items()}
    hist = take["r_history_features"].reshape(2, BATCHES, 4, SEQ, FEAT).transpose(1, 4, 0, 2, 3)
    hist = np.ascontiguousarray(hist).reshape(BATCHES, FEAT, 2 * 4 * SEQ)
    cand = np.ascontiguousarray(take["r_candidate_features"].T)
    length = take["r_history_length"]
    lens = np.zeros((128, HALF + SUPERBLOCKS), length.dtype)
    lens[0:64, 0:HALF] = length[0:HALF]
    lens[64:128, 0:HALF] = length[HALF:USERS]
    rows = length.reshape(2, SUPERBLOCKS, SB_BATCHES, 4).transpose(3, 2, 0, 1).reshape(4, USER_ROWS, SUPERBLOCKS)
    row_view = lens[:, HALF:].reshape(4, 32, SUPERBLOCKS)
    for copy in range(COPIES):
        row_view[:, USER_ROWS * copy:USER_ROWS * (copy + 1)] = rows
    lens[:, HALF:] = row_view.reshape(128, SUPERBLOCKS)
    params = np.zeros((128, PARAMS), np.float32)

    def put(name, value, column=0, halves=1):
        at = PARAM_COLS[name][0] + column
        value = value.reshape(value.shape[0], -1)
        n, width = value.shape
        for h in range(halves):
            params[64 * h:64 * h + n, at:at + width] = value

    put("wi", take["L0_rec_Wi"])
    put("wiT", take["L0_rec_Wi"].T)
    for name, source in (("wk", "Wk"), ("wq", "Wq"), ("bi", "bi"), ("wv", "Wv")):
        put(name, take[f"L0_rec_{source}"], halves=2)
    row_copy = np.arange(128) % 32 // USER_ROWS
    put("keep1", (row_copy >= 1).astype(np.float32))
    put("keep2", (row_copy >= 2).astype(np.float32))
    for c in range(3):
        put("w1", take["L0_rec_W1"][EMB * c:EMB * (c + 1)], c * HID1, halves=2)
    put("w2", take["L0_rec_W2"])
    put("w3", take["L0_rec_W3"])
    put("wo", take["L0_rec_Wo"])
    put("bo", take["L0_rec_bo"])
    for layer in range(3):
        for name in ("b", "g", "be", "m", "v"):
            put(name, take[f"L0_rec_{name}{layer + 1}"], layer)

    nc = bacc.Bacc("TRN2", target_bir_lowering=False, num_devices=1)
    arrays = {"history_dram": hist, "candidates_dram": cand, "parameters_dram": params, "lengths_dram": lens}
    aps = [nc.dram_tensor(name, a.shape, mybir.dt.from_np(a.dtype), kind="ExternalInput").ap()
           for name, a in arrays.items()]
    out = nc.dram_tensor("probability", (USERS,), F32, kind="ExternalOutput").ap()
    build(nc, *aps, out)
    return run_bass_kernel_spmd(nc, [arrays], core_ids=[0]).results[0]["probability"]
```

```python
from contextlib import ExitStack

import concourse.bass as bass
from concourse import mybir

F32 = mybir.dt.float32
BF16 = mybir.dt.bfloat16
I32 = mybir.dt.int32
ALU = mybir.AluOpType
ACT = mybir.ActivationFunctionType
AX_X = mybir.AxisListType.X

USERS, SEQ, FEAT, EMB = 512, 200, 128, 64
HID1, HID2, HID3 = 128, 64, 32
BN_EPS = 1e-05
MASKED = -1000000000.0

HALF = USERS // 2
QUADS = HALF // 2
QCOLS = 2 * SEQ
BATCHES = HALF // 4
SB_PAIRS = 8
SB_QUADS = SB_PAIRS // 2
SB_BATCHES = SB_PAIRS // 4
SUPERBLOCKS = HALF // SB_PAIRS
BODY_QUADS = 16
BODY_PAIRS = 2 * BODY_QUADS
BODY_BATCHES = BODY_QUADS // 2
BODY_SBS = BODY_QUADS // SB_QUADS
BODIES = QUADS // BODY_QUADS
MLP_PARTS = (slice(0, HALF - BODY_PAIRS), slice(HALF - BODY_PAIRS, HALF))
LOAD_SLOTS = 4
HID_SLOTS = 8
DELAY = 9
COPIES = 3
USER_ROWS = 2 * SB_BATCHES

PARAM_COLS = {}
_at = 0
for _name, _width in (("wi", EMB), ("wiT", FEAT), ("wk", EMB), ("wq", EMB), ("bi", 1), ("wv", 1),
                      ("keep1", 1), ("keep2", 1), ("w1", 3 * HID1), ("w2", HID2), ("w3", HID3), ("wo", 1),
                      ("bo", 1), ("b", 3), ("g", 3), ("be", 3), ("m", 3), ("v", 3)):
    PARAM_COLS[_name] = (_at, _width)
    _at += _width
PARAMS = _at
WK_WQ = slice(PARAM_COLS["wk"][0], PARAM_COLS["wq"][0] + EMB)
EARLY = PARAM_COLS["w1"][0]


def build(nc, hist_dram, cand_dram, params_dram, lens_dram, out_dram):
    with ExitStack() as ctx:
        def sb(name, shape, dt=F32):
            return ctx.enter_context(nc.sbuf_tensor(name, shape, dt))

        def psum(name, shape):
            return ctx.enter_context(nc.psum_tensor(name, shape, F32))

        def sem(name):
            return ctx.enter_context(nc.semaphore(name))

        params = sb("params", [128, PARAMS])

        def param(name, rows=slice(0, 128)):
            at, width = PARAM_COLS[name]
            return params[rows, at:at + width]

        history = sb("history", [128, LOAD_SLOTS, 2, 4, SEQ])
        candT = sb("candT", [128, USERS])
        lens_raw = sb("lens_raw", [128, HALF + SUPERBLOCKS], I32)
        lens = sb("lens", [128, HALF + SUPERBLOCKS])
        pair_len = lens[:, 0:HALF]
        row_len = lens[:, HALF:HALF + SUPERBLOCKS]
        folded = sb("folded", [128, 2 * EMB])
        wv_rows = sb("wv_rows", [128, SB_BATCHES, 32])
        cand = sb("cand", [128, HALF])
        query_bias = sb("query_bias", [128, 1])
        query = sb("query", [128, HALF])
        query_now = sb("query_now", [128, BODY_PAIRS])
        len_now = sb("len_now", [128, BODY_PAIRS])
        rowlen_now = sb("rowlen_now", [128, BODY_SBS])
        item = sb("item", [128, SEQ])
        spread = sb("spread", [128, SB_PAIRS, 2, EMB], BF16)
        hidden = sb("hidden", [128, HID_SLOTS, QCOLS])
        kept = sb("kept", [128, BODY_QUADS, 2, SEQ])
        scratch = sb("scratch", [128, 2, 2, SEQ])
        valid = sb("valid", [128, SEQ], I32)
        scores = sb("scores", [128, SEQ])
        neg_max = sb("neg_max", [128, 1])
        weights = sb("weights", [128, SEQ])
        weight_sum = sb("weight_sum", [128, 1])
        inv_sum = sb("inv_sum", [128, 1])
        part_a = sb("part_a", [128, SEQ], BF16)
        part_b = sb("part_b", [128, SEQ], BF16)
        attn = sb("attn", [128, SEQ])
        rest = sb("rest", [128, SEQ])
        parts = sb("parts", [128, 2, SEQ], BF16)
        sum_now = sb("sum_now", [128, BODY_PAIRS])
        interest_now = sb("interest_now", [128, BODY_PAIRS])
        hist_sum = sb("hist_sum", [128, HALF])
        interest = sb("interest", [128, HALF])
        average = sb("average", [128, HALF])
        inv_len = sb("inv_len", [128, HALF])
        count = sb("count", [128, HALF])
        bn_scale = sb("bn_scale", [128, 3])
        bn_shift = sb("bn_shift", [128, 3])
        bn_power = sb("bn_power", [128, 3])
        x1 = sb("x1", [HID1, 2, HALF])
        x2 = sb("x2", [HID2, 2, HALF])
        x3 = sb("x3", [HID3, 2, HALF])
        result = sb("result", [1, 2, HALF])

        key_ps = psum("key_ps", [128, 2, 512])
        hist_ps = psum("hist_ps", [128, 2, 512])
        score_ps = psum("score_ps", [128, 2, 512])
        attn_ps = psum("attn_ps", [128, 2, 512])
        w1 = param("w1").rearrange("p (c n) -> p c n", c=3)
        z1, z2, z3, z4 = (score_ps[0:n, 0, :].rearrange("p (h n) -> p h n", h=2) for n in (HID1, HID2, HID3, 1))
        z1 = (z1, key_ps[:, :, 0:HALF])

        early_landed = sem("early_landed")
        late_landed = sem("late_landed")
        cand_landed = sem("cand_landed")
        lens_landed = sem("lens_landed")
        batch_landed = [sem(f"batch_landed{i}") for i in range(LOAD_SLOTS)]
        first_quad_landed = sem("first_quad_landed")
        item_made = sem("item_made")
        spread_made = sem("spread_made")
        wv_steps = sem("wv_steps")
        wv_ready = sem("wv_ready")
        lens_ready = sem("lens_ready")
        folded_product = sem("folded_product")
        folded_ready = sem("folded_ready")
        bias_product = sem("bias_product")
        bias_ready = sem("bias_ready")
        cand_product = sem("cand_product")
        cand_ready = sem("cand_ready")
        query_product = sem("query_product")
        query_ready = sem("query_ready")
        query_staged = sem("query_staged")
        len_staged = sem("len_staged")
        rowlen_staged = sem("rowlen_staged")
        key_ready = sem("key_ready")
        hist_ready = sem("hist_ready")
        relu_done = sem("relu_done")
        masked_summed = sem("masked_summed")
        scored = sem("scored")
        mask_ready = sem("mask_ready")
        scores_taken = sem("scores_taken")
        max_ready = sem("max_ready")
        exp_done = sem("exp_done")
        inv_ready = sem("inv_ready")
        split_steps = sem("split_steps")
        parts_ready = sem("parts_ready")
        attn_spread = sem("attn_spread")
        attn_summed = sem("attn_summed")
        sums_stored = sem("sums_stored")
        bn_steps = sem("bn_steps")
        bn_ready = sem("bn_ready")
        mean_steps = sem("mean_steps")
        features_ready = sem("features_ready")
        z1_ready = sem("z1_ready")
        x1_ready = sem("x1_ready")
        z2_ready = sem("z2_ready")
        x2_ready = sem("x2_ready")
        z3_ready = sem("z3_ready")
        x3_ready = sem("x3_ready")
        z4_ready = sem("z4_ready")
        result_ready = sem("result_ready")
        result_stored = sem("result_stored")

        block = ctx.enter_context(nc.Block())

        def wait(eng, semaphore, value):
            if not isinstance(value, int) or value > 0:
                eng.wait_ge(semaphore, value)

        def wait_apart(eng, *waits):
            waits = [(s, v if isinstance(v, int) else eng.to_reg(v)) for s, v in waits]
            eng.wait_ge(lens_ready, 1)
            for semaphore, value in waits:
                wait(eng, semaphore, value)

        @block.sync
        def _(sp):
            def load(t, batch):
                wait(sp, hist_ready, 2 * (BODY_BATCHES * t + batch - LOAD_SLOTS + 1))
                slot = batch % LOAD_SLOTS
                sp.dma_start(history[:, slot, :, :, :].rearrange("f h p s -> f (h p s)"),
                             hist_dram[bass.ds(BODY_BATCHES * t + batch, 1), :, :].rearrange("a f c -> (a f) c"))\
                  .then_inc(batch_landed[slot], 16)

            first = hist_dram[0, :, :].rearrange("f (h p s) -> f h p s", h=2, p=4)
            sp.dma_start(params[:, 0:EARLY], params_dram[:, 0:EARLY]).then_inc(early_landed, 16)
            sp.dma_start(history[:, 0, :, 0:2, :], first[:, :, 0:2, :]).then_inc(first_quad_landed, 16)
            sp.dma_start(candT[:, :], cand_dram).then_inc(cand_landed, 16)
            sp.dma_start(history[:, 0, :, 2:4, :], first[:, :, 2:4, :]).then_inc(batch_landed[0], 16)
            sp.dma_start(lens_raw[:, :], lens_dram).then_inc(lens_landed, 16)
            for batch in range(1, BODY_BATCHES):
                load(0, batch)
                if batch == LOAD_SLOTS - 1:
                    sp.dma_start(params[:, EARLY:PARAMS], params_dram[:, EARLY:PARAMS]).then_inc(late_landed, 16)
            with sp.Fori(1, BODIES) as t:
                for batch in range(BODY_BATCHES):
                    load(t, batch)
            sp.wait_ge(result_ready, 2)
            sp.dma_start(out_dram.rearrange("(a n) -> a n", a=1), result[:, :, :].rearrange("a h n -> a (h n)")).then_inc(result_stored, 16)
            sp.wait_ge(result_stored, 16)

        @block.gpsimd
        def _(pool):
            pool.iota(item[:, :], pattern=[[1, SEQ]], base=0, channel_multiplier=0,
                      allow_small_or_imprecise_dtypes=True).then_inc(item_made, 1)
            pool.memset(wv_rows[:, :, :], 0.0).then_inc(wv_steps, 1)
            pool.wait_ge(wv_steps, 1)
            wv_view = wv_rows[:, :, :].rearrange("p k (c u) -> p k c u", u=USER_ROWS)
            for h in range(2):
                v = wv_view[64 * h:64 * h + 64, :, 0:COPIES, :]
                pool.affine_select(out=v, in_=v, compare_op=ALU.not_equal, fill=1.0, base=h,
                                   pattern=[[2, SB_BATCHES], [0, COPIES], [-1, USER_ROWS]],
                                   channel_multiplier=0).then_inc(wv_steps, 1)
            pool.wait_ge(wv_steps, 3)
            pool.wait_ge(early_landed, 16)
            pool.tensor_scalar(wv_rows[:, :, :], wv_rows[:, :, :], param("wv"), None, ALU.mult).then_inc(wv_ready, 1)

            flat = spread[:, :, :, :].rearrange("p (k q) h e -> p k q (h e)", q=4)
            pool.memset(spread[:, :, :, :], 0.0).then_inc(spread_made, 1)
            for copy in range(COPIES):
                for h in range(2):
                    v = flat[:, :, :, EMB * h:EMB * h + EMB]
                    if h == 0:
                        pool.wait_ge(spread_made, 2 * copy + 1)
                    pool.affine_select(out=v, in_=v, compare_op=ALU.not_equal, fill=1.0,
                                       base=-USER_ROWS * copy - h, pattern=[[-2, SB_BATCHES], [-32, 4], [0, EMB]],
                                       channel_multiplier=1).then_inc(spread_made, 1)

            pool.wait_ge(lens_ready, 1)

            def prepare(t, j):
                superblock = BODY_SBS * t + j
                wait_apart(pool, (exp_done, superblock))
                if j == 0:
                    wait(pool, mask_ready, 2 * superblock)
                    pool.tensor_copy(rowlen_now[:, :], row_len[:, bass.ds(superblock, BODY_SBS)]).then_inc(rowlen_staged, 1)
                pool.memset(scores[:, :], MASKED).then_inc(mask_ready, 1)
                wait_apart(pool, (rowlen_staged, t + 1))
                pool.tensor_scalar(valid[:, :], item[:, :], rowlen_now[:, j:j + 1], None,
                                   ALU.is_lt).then_inc(mask_ready, 1)

            def split(t, j):
                superblock = BODY_SBS * t + j
                done = 4 * superblock
                wait_apart(pool, (inv_ready, superblock + 1), (parts_ready, superblock))
                pool.tensor_scalar(attn[:, :], weights[:, :], inv_sum[:, 0:1], 1.0,
                                   ALU.mult, ALU.mult).then_inc(split_steps, 1)
                pool.tensor_scalar(part_a[:, :], weights[:, :], inv_sum[:, 0:1], param("keep1"),
                                   ALU.mult, ALU.mult).then_inc(split_steps, 1)
                wait(pool, split_steps, done + 2)
                pool.tensor_tensor(rest[:, :], attn[:, :], part_a[:, :], ALU.subtract).then_inc(split_steps, 1)
                wait_apart(pool, (split_steps, done + 3))
                pool.tensor_scalar(part_b[:, :], rest[:, :], param("keep2"), 1.0,
                                   ALU.mult, ALU.mult).then_inc(split_steps, 1)
                wait(pool, split_steps, done + 4)
                wait(pool, attn_spread, SB_QUADS * (superblock - 1))
                pool.tensor_tensor(parts[:, j % 2, :], rest[:, :], part_b[:, :],
                                   ALU.subtract).then_inc(parts_ready, 1)

            def body(t, last=False):
                for j in range(BODY_SBS):
                    if last and j == BODY_SBS - 1:
                        return
                    split(t, j)
                    if j < BODY_SBS - 1:
                        prepare(t, j + 1)
                    else:
                        prepare(t + 1, 0)

            prepare(0, 0)
            pool.wait_ge(late_landed, 16)
            pool.memset(bn_power[:, :], -0.5).then_inc(bn_steps, 1)
            pool.tensor_scalar(bn_scale[:, :], param("v"), BN_EPS, None, ALU.add).then_inc(bn_steps, 1)
            pool.tensor_tensor(bn_shift[:, :], param("b"), param("m"), ALU.subtract).then_inc(bn_steps, 1)
            pool.wait_ge(bn_steps, 3)
            pool.tensor_tensor(bn_scale[:, :], bn_scale[:, :], bn_power[:, :], ALU.pow).then_inc(bn_steps, 1)
            pool.wait_ge(bn_steps, 4)
            pool.tensor_tensor(bn_scale[:, :], bn_scale[:, :], param("g"), ALU.mult).then_inc(bn_steps, 1)
            pool.wait_ge(bn_steps, 5)
            pool.tensor_tensor(bn_shift[:, :], bn_shift[:, :], bn_scale[:, :], ALU.mult).then_inc(bn_steps, 1)
            pool.wait_ge(bn_steps, 6)
            pool.tensor_tensor(bn_shift[:, :], bn_shift[:, :], param("be"), ALU.add).then_inc(bn_ready, 1)
            body(0)
            with pool.Fori(1, BODIES - 1) as t:
                body(t)
            body(BODIES - 1, True)

        @block.scalar
        def _(act):
            def relu_quad(t, r):
                g = BODY_QUADS * t + r
                wait(act, key_ready, g + 1)
                if r % SB_QUADS == 0:
                    wait(act, scored, (BODY_QUADS * t + r - HID_SLOTS) // SB_QUADS + 1 if isinstance(t, int)
                         else BODY_SBS * t + (r - HID_SLOTS) // SB_QUADS + 1)
                for u in range(2):
                    act.activation(hidden[:, r % HID_SLOTS, u * SEQ:(u + 1) * SEQ],
                                   key_ps[:, r % 2, u * SEQ:(u + 1) * SEQ], ACT.Relu,
                                   bias=query_now[:, 2 * r + u:2 * r + u + 1]).then_inc(relu_done, 1)

            def exponent(s):
                wait(act, max_ready, s + 1)
                wait(act, split_steps, 4 * s)
                act.activation(weights[:, :], scores[:, :], ACT.Exp, bias=neg_max[:, 0:1],
                               accum_out=weight_sum[:, 0:1]).then_inc(exp_done, 1)

            def body(t):
                wait(act, relu_done, BODY_PAIRS * t)
                act.activation(query_now[:, :], query[:, bass.ds(BODY_PAIRS * t, BODY_PAIRS)],
                               ACT.Copy).then_inc(query_staged, 1)
                wait(act, query_staged, t + 1)
                for r in range(BODY_QUADS):
                    relu_quad(t, r)
                    if r % SB_QUADS == 1 and (r > 1 or not (isinstance(t, int) and t == 0)):
                        exponent(BODY_SBS * t + r // SB_QUADS - 1)

            def mlp_stage(n, stage):
                pairs = MLP_PARTS[n]
                if stage == 1:
                    act.wait_ge(bn_ready, 1)
                    act.wait_ge(z1_ready, 2 * (n + 1))
                    act.activation(x1[:, :, pairs], z1[n][:, :, pairs], ACT.Relu, bias=bn_shift[:, 0:1],
                                   scale=bn_scale[:, 0:1]).then_inc(x1_ready, 1)
                if stage == 2:
                    act.wait_ge(z2_ready, n + 1)
                    act.activation(x2[:, :, pairs], z2[:, :, pairs], ACT.Relu, bias=bn_shift[0:HID2, 1:2],
                                   scale=bn_scale[0:HID2, 1:2]).then_inc(x2_ready, 1)
                if stage == 3:
                    act.wait_ge(z3_ready, n + 1)
                    act.activation(x3[:, :, pairs], z3[:, :, pairs], ACT.Relu, bias=bn_shift[0:HID3, 2:3],
                                   scale=bn_scale[0:HID3, 2:3]).then_inc(x3_ready, 1)
                if stage == 4:
                    act.wait_ge(z4_ready, n + 1)
                    act.activation(result[:, :, pairs], z4[:, :, pairs], ACT.Sigmoid,
                                   bias=param("bo", slice(0, 1))).then_inc(result_ready, 1)

            act.wait_ge(query_ready, 1)
            body(0)
            with act.Fori(1, BODIES) as t:
                body(t)
            mlp_stage(0, 1)
            exponent(SUPERBLOCKS - 1)
            mlp_stage(0, 2)

            for stage in (3, 4):
                mlp_stage(0, stage)
            for stage in range(1, 5):
                mlp_stage(1, stage)

        @block.tensor
        def _(pe):
            pe.wait_ge(early_landed, 16)
            pe.matmul(attn_ps[:, 0, 0:2 * EMB], param("wiT", slice(0, EMB)), params[0:EMB, WK_WQ],
                      start=True, stop=True).then_inc(folded_product, 1)
            for h in range(2):
                for name in ("wk", "wq"):
                    product = pe.matmul(attn_ps[64 * h:64 * h + 64, 1, 0:1], param(name, slice(0, EMB)),
                                        param("bi", slice(0, EMB)), start=(name == "wk"), stop=(name == "wq"))
            product.then_inc(bias_product, 1)

            def queries():
                pe.wait_ge(cand_landed, 16)
                for h in range(2):
                    product = pe.matmul(score_ps[64 * h:64 * h + 64, 0, 0:HALF], folded[:, EMB:2 * EMB],
                                        candT[:, h * HALF:(h + 1) * HALF], start=True, stop=True)
                product.then_inc(query_product, 1)

            def candidates():
                pe.wait_ge(bias_ready, 1)
                for h in range(2):
                    product = pe.matmul(attn_ps[64 * h:64 * h + 64, 1, 0:HALF], param("wi"),
                                        candT[:, h * HALF:(h + 1) * HALF], start=True, stop=True)
                product.then_inc(cand_product, 1)

            def project(t, r):
                g = BODY_QUADS * t + r
                batch, pair = r // 2, 2 * (r % 2)
                slot = batch % LOAD_SLOTS
                if isinstance(t, int) and t == 0 and r == 0:
                    pe.wait_ge(first_quad_landed, 16)
                elif r % 2 == 0 or (isinstance(t, int) and t == 0 and r == 1):
                    wait(pe, batch_landed[slot], 16 * (BODY_BATCHES // LOAD_SLOTS * t + batch // LOAD_SLOTS + 1))
                items = [history[:, slot, h, pair:pair + 2, :].rearrange("f p s -> f (p s)") for h in range(2)]
                wait(pe, relu_done, 2 * (g - 2) + 2)
                pe.matmul(key_ps[0:64, r % 2, 0:QCOLS], folded[:, 0:EMB], items[0], start=True, stop=True)
                pe.matmul(key_ps[64:128, r % 2, 0:QCOLS], folded[:, 0:EMB], items[1], start=True, stop=True).then_inc(key_ready, 1)
                wait(pe, masked_summed, 2 * (g - 2) + 2)
                pe.matmul(hist_ps[0:64, r % 2, 0:QCOLS], param("wi"), items[0], start=True, stop=True)
                pe.matmul(hist_ps[64:128, r % 2, 0:QCOLS], param("wi"), items[1], start=True, stop=True).then_inc(hist_ready, 1)

            def score(t, r):
                first_quad = (r - SB_QUADS) % BODY_QUADS
                bank = first_quad // SB_QUADS % 2
                wait(pe, relu_done, 2 * (BODY_QUADS * t + r))
                wait(pe, scores_taken, BODY_SBS * t + r // SB_QUADS - 2)
                for k in range(SB_BATCHES):
                    for q in range(4):
                        quad = first_quad + 2 * k + q // 2
                        product = pe.matmul(score_ps[32 * q:32 * q + 32, bank, 0:SEQ], wv_rows[:, k, :],
                                            hidden[:, quad % HID_SLOTS, (q % 2) * SEQ:(q % 2 + 1) * SEQ],
                                            start=(k == 0), stop=(k == SB_BATCHES - 1))
                product.then_inc(scored, 1)

            def spread_attn(t, r):
                at = r - DELAY
                quad = at % BODY_QUADS
                if quad % SB_QUADS == 0:
                    wait(pe, parts_ready, BODY_SBS * t + at // SB_QUADS + 1)
                wait(pe, attn_summed, 2 * (BODY_QUADS * t + at - 2) + 2)
                for u in range(2):
                    pair = 2 * (quad % SB_QUADS) + u
                    product = pe.matmul(attn_ps[:, quad % 2, u * SEQ:(u + 1) * SEQ],
                                        spread[:, pair, :, :].rearrange("p h e -> p (h e)"),
                                        parts[:, quad // SB_QUADS % 2, :], start=True, stop=True)
                product.then_inc(attn_spread, 1)

            def mlp_stage(n, stage):
                pairs = MLP_PARTS[n]
                if stage == 0:
                    pe.wait_ge(late_landed, 16)
                    pe.wait_ge(features_ready, n + 1)
                    pe.wait_ge(scores_taken, SUPERBLOCKS - 1)
                    wait(pe, result_ready, n)
                if stage == 1 and n == 0:
                    pe.wait_ge(z1_ready, 1)
                if stage < 2:
                    rows = slice(64 * stage, 64 * stage + 64)
                    for c, x in enumerate((interest, cand, average)):
                        product = pe.matmul(z1[n][:, stage, pairs], w1[rows, c, :], x[rows, pairs],
                                            start=(c == 0), stop=(c == 2), skip_group_check=True)
                    product.then_inc(z1_ready, 1)
                if stage == 2:
                    pe.wait_ge(x1_ready, n + 1)
                    pe.matmul(z2[:, :, pairs], param("w2"), x1[:, :, pairs], start=True, stop=True).then_inc(z2_ready, 1)
                if stage == 3:
                    pe.wait_ge(x2_ready, n + 1)
                    pe.matmul(z3[:, :, pairs], param("w3", slice(0, HID2)), x2[:, :, pairs],
                              start=True, stop=True).then_inc(z3_ready, 1)
                if stage == 4:
                    pe.wait_ge(x3_ready, n + 1)
                    pe.matmul(z4[:, :, pairs], param("wo", slice(0, HID3)), x3[:, :, pairs],
                              start=True, stop=True).then_inc(z4_ready, 1)

            def body(t, last=False):
                for r in range(BODY_QUADS):
                    started = not isinstance(t, int) or BODY_QUADS * t + r >= SB_QUADS
                    first = isinstance(t, int) and t == 0
                    project(t, r)
                    if first and r == 0:
                        queries()
                    if first and r == 2:
                        candidates()
                    if first and r == SB_QUADS:
                        pe.wait_ge(wv_ready, 1)
                    if first and r == DELAY:
                        pe.wait_ge(cand_ready, 1)
                        pe.wait_ge(spread_made, 1 + 2 * COPIES)
                    if r % SB_QUADS == 0 and started:
                        score(t, r)
                    if not isinstance(t, int) or BODY_QUADS * t + r >= DELAY:
                        spread_attn(t, r)
                    if last and r >= BODY_QUADS - 2:
                        mlp_stage(0, r - BODY_QUADS + 2)

            pe.wait_ge(folded_ready, 1)
            body(0)
            with pe.Fori(1, BODIES - 1) as t:
                body(t)
            body(BODIES - 1, last=True)
            score(BODIES, 0)
            for r in range(DELAY):
                spread_attn(BODIES, r)
                if r in (0, 1, 3):
                    mlp_stage(0, 2 + (r + 1) // 2)
            for stage in range(5):
                mlp_stage(1, stage)

        @block.vector
        def _(dve):
            dve.wait_ge(folded_product, 1)
            dve.tensor_copy(folded[:, :], attn_ps[:, 0, 0:2 * EMB]).then_inc(folded_ready, 1)
            dve.wait_ge(bias_product, 1)
            dve.tensor_copy(query_bias[:, :], attn_ps[:, 1, 0:1]).then_inc(bias_ready, 1)
            dve.wait_ge(bias_ready, 1)
            dve.wait_ge(query_product, 1)
            dve.tensor_scalar(query[:, :], score_ps[:, 0, 0:HALF], query_bias[:, 0:1], None,
                              ALU.add).then_inc(query_ready, 1)
            dve.wait_ge(lens_landed, 16)
            dve.tensor_copy(lens[:, :], lens_raw[:, :]).then_inc(lens_ready, 1)
            dve.wait_ge(item_made, 1)
            dve.wait_ge(lens_ready, 1)
            dve.tensor_scalar(count[:, :], pair_len, float(SEQ), 0.0, ALU.min, ALU.max).then_inc(mean_steps, 1)

            def masked_sum(t, r):
                wait(dve, hist_ready, BODY_QUADS * t + r + 1)
                for u in range(2):
                    col = 2 * r + u
                    dve.scalar_tensor_tensor(out=kept[:, r, u, :], in0=item[:, :], scalar=len_now[:, col:col + 1],
                                             in1=hist_ps[:, r % 2, u * SEQ:(u + 1) * SEQ], op0=ALU.is_lt, op1=ALU.mult,
                                             accum_out=sum_now[:, col:col + 1]).then_inc(masked_summed, 1)

            def attended_sum(t, r):
                at = r - DELAY
                quad = at % BODY_QUADS
                wait(dve, attn_spread, BODY_QUADS * t + at + 1)
                wait(dve, attn_summed, 2 * (BODY_QUADS * t + at - 1))
                for u in range(2):
                    col = 2 * quad + u
                    dve.tensor_tensor_reduce(scratch[:, quad % 2, u, :], attn_ps[:, quad % 2, u * SEQ:(u + 1) * SEQ],
                                             kept[:, quad, u, :], 1.0, 0.0, ALU.mult, ALU.add,
                                             interest_now[:, col:col + 1]).then_inc(attn_summed, 1)

            def maximum(s, bank):
                wait_apart(dve, (scored, s + 1), (mask_ready, 2 * (s + 1)))
                dve.copy_predicated(scores[:, :], valid[:, :], score_ps[:, bank, 0:SEQ]).then_inc(scores_taken, 1)
                wait(dve, scores_taken, s + 1)
                dve.reduce_max(neg_max[:, 0:1], scores[:, :], AX_X, negate=True).then_inc(max_ready, 1)

            def invert(s):
                wait(dve, exp_done, s + 1)
                dve.reciprocal(inv_sum[:, 0:1], weight_sum[:, 0:1]).then_inc(inv_ready, 1)

            def store_interest(t, stored=sums_stored):
                wait(dve, attn_summed, BODY_PAIRS * (t + 1))
                dve.tensor_scalar(interest[:, bass.ds(BODY_PAIRS * t, BODY_PAIRS)], interest_now[:, :], param("bi"),
                                  None, ALU.add).then_inc(stored, 1)

            def mean(n):
                pairs = MLP_PARTS[n]
                dve.wait_ge(mean_steps, 2 + n)
                dve.wait_ge(sums_stored, 2 * BODIES - 2 + n)
                dve.scalar_tensor_tensor(out=average[:, pairs], in0=count[:, pairs], scalar=param("bi"),
                                         in1=hist_sum[:, pairs], op0=ALU.mult, op1=ALU.add).then_inc(mean_steps, 1)
                dve.wait_ge(mean_steps, 3 + n)
                dve.tensor_tensor(average[:, pairs], average[:, pairs], inv_len[:, pairs],
                                  ALU.mult).then_inc(features_ready if n == 0 else mean_steps, 1)

            def body(t, last=False):
                started = not (isinstance(t, int) and t == 0)
                wait(dve, sums_stored, 2 * t - 1)
                dve.tensor_copy(len_now[:, :], pair_len[:, bass.ds(BODY_PAIRS * t, BODY_PAIRS)]).then_inc(len_staged, 1)
                wait(dve, len_staged, t + 1)
                for r in range(BODY_QUADS):
                    j = r // SB_QUADS - 1
                    if r % SB_QUADS == 1 and (started or j >= 0):
                        maximum(BODY_SBS * t + j, j % 2)
                    if r % SB_QUADS == 2 and (started or j >= 0):
                        invert(BODY_SBS * t + j)
                    masked_sum(t, r)
                    if not started and r == 2:
                        dve.wait_ge(cand_product, 1)
                        dve.wait_ge(early_landed, 16)
                        dve.tensor_scalar(cand[:, :], attn_ps[:, 1, 0:HALF], param("bi"), None,
                                          ALU.add).then_inc(cand_ready, 1)
                    if not started and r == SB_QUADS:
                        dve.reciprocal(inv_len[:, :], pair_len).then_inc(mean_steps, 1)
                    if last and r == DELAY:
                        mean(0)
                    if started and r == DELAY:
                        wait(dve, sums_stored, 2 * t)
                    if started or r >= DELAY:
                        attended_sum(t, r)
                    if started and r == DELAY - 1:
                        store_interest(t - 1)
                wait(dve, masked_summed, BODY_PAIRS * (t + 1))
                dve.tensor_copy(hist_sum[:, bass.ds(BODY_PAIRS * t, BODY_PAIRS)], sum_now[:, :]).then_inc(sums_stored, 1)

            body(0)
            with dve.Fori(1, BODIES - 1) as t:
                body(t)
            body(BODIES - 1, last=True)

            mean(1)
            maximum(SUPERBLOCKS - 1, 1)
            attended_sum(BODIES, 0)
            invert(SUPERBLOCKS - 1)
            dve.wait_ge(parts_ready, SUPERBLOCKS - 1)
            dve.wait_ge(inv_ready, SUPERBLOCKS)
            dve.tensor_scalar(attn[:, :], weights[:, :], inv_sum[:, 0:1], None, ALU.mult).then_inc(split_steps, 1)
            dve.tensor_scalar(part_a[:, :], weights[:, :], inv_sum[:, 0:1], param("keep1"),
                              ALU.mult, ALU.mult).then_inc(split_steps, 1)
            dve.wait_ge(split_steps, 4 * SUPERBLOCKS - 2)
            dve.tensor_tensor(rest[:, :], attn[:, :], part_a[:, :], ALU.subtract).then_inc(split_steps, 1)
            dve.wait_ge(split_steps, 4 * SUPERBLOCKS - 1)
            dve.tensor_scalar(part_b[:, :], rest[:, :], param("keep2"), None, ALU.mult).then_inc(split_steps, 1)
            dve.wait_ge(split_steps, 4 * SUPERBLOCKS)
            dve.wait_ge(attn_spread, SB_QUADS * (SUPERBLOCKS - 2))
            dve.tensor_tensor(parts[:, (BODY_SBS - 1) % 2, :], rest[:, :], part_b[:, :],
                              ALU.subtract).then_inc(parts_ready, 1)
            for r in range(1, DELAY):
                attended_sum(BODIES, r)
            dve.wait_ge(mean_steps, 5)
            store_interest(BODIES - 1, features_ready)


def kernel(**inputs):
    import numpy as np
    import concourse.bacc as bacc
    from concourse.bass_utils import run_bass_kernel_spmd

    take = {name: np.ascontiguousarray(value) for name, value in inputs.items()}
    hist = take["r_history_features"].reshape(2, BATCHES, 4, SEQ, FEAT).transpose(1, 4, 0, 2, 3)
    hist = np.ascontiguousarray(hist).reshape(BATCHES, FEAT, 2 * 4 * SEQ)
    cand = np.ascontiguousarray(take["r_candidate_features"].T)
    length = take["r_history_length"]
    lens = np.zeros((128, HALF + SUPERBLOCKS), length.dtype)
    lens[0:64, 0:HALF] = length[0:HALF]
    lens[64:128, 0:HALF] = length[HALF:USERS]
    rows = length.reshape(2, SUPERBLOCKS, SB_BATCHES, 4).transpose(3, 2, 0, 1).reshape(4, USER_ROWS, SUPERBLOCKS)
    row_view = lens[:, HALF:].reshape(4, 32, SUPERBLOCKS)
    for copy in range(COPIES):
        row_view[:, USER_ROWS * copy:USER_ROWS * (copy + 1)] = rows
    lens[:, HALF:] = row_view.reshape(128, SUPERBLOCKS)
    params = np.zeros((128, PARAMS), np.float32)

    def put(name, value, column=0, halves=1):
        at = PARAM_COLS[name][0] + column
        value = value.reshape(value.shape[0], -1)
        n, width = value.shape
        for h in range(halves):
            params[64 * h:64 * h + n, at:at + width] = value

    put("wi", take["L0_rec_Wi"])
    put("wiT", take["L0_rec_Wi"].T)
    for name, source in (("wk", "Wk"), ("wq", "Wq"), ("bi", "bi"), ("wv", "Wv")):
        put(name, take[f"L0_rec_{source}"], halves=2)
    row_copy = np.arange(128) % 32 // USER_ROWS
    put("keep1", (row_copy >= 1).astype(np.float32))
    put("keep2", (row_copy >= 2).astype(np.float32))
    for c in range(3):
        put("w1", take["L0_rec_W1"][EMB * c:EMB * (c + 1)], c * HID1, halves=2)
    put("w2", take["L0_rec_W2"])
    put("w3", take["L0_rec_W3"])
    put("wo", take["L0_rec_Wo"])
    put("bo", take["L0_rec_bo"])
    for layer in range(3):
        for name in ("b", "g", "be", "m", "v"):
            put(name, take[f"L0_rec_{name}{layer + 1}"], layer)

    nc = bacc.Bacc("TRN2", target_bir_lowering=False, num_devices=1)
    arrays = {"history_dram": hist, "candidates_dram": cand, "parameters_dram": params, "lengths_dram": lens}
    aps = [nc.dram_tensor(name, a.shape, mybir.dt.from_np(a.dtype), kind="ExternalInput").ap()
           for name, a in arrays.items()]
    out = nc.dram_tensor("probability", (USERS,), F32, kind="ExternalOutput").ap()
    build(nc, *aps, out)
    return run_bass_kernel_spmd(nc, [arrays], core_ids=[0]).results[0]["probability"]
```

```python
from contextlib import ExitStack

import concourse.bass as bass
from concourse import mybir

F32 = mybir.dt.float32
BF16 = mybir.dt.bfloat16
I32 = mybir.dt.int32
ALU = mybir.AluOpType
ACT = mybir.ActivationFunctionType
AX_X = mybir.AxisListType.X

USERS, SEQ, FEAT, EMB = 512, 200, 128, 64
HID1, HID2, HID3 = 128, 64, 32
BN_EPS = 1e-05
MASKED = -1000000000.0

HALF = USERS // 2
QUADS = HALF // 2
QCOLS = 2 * SEQ
BATCHES = HALF // 4
SB_PAIRS = 8
SB_QUADS = SB_PAIRS // 2
SB_BATCHES = SB_PAIRS // 4
SUPERBLOCKS = HALF // SB_PAIRS
BODY_QUADS = 16
BODY_PAIRS = 2 * BODY_QUADS
BODY_BATCHES = BODY_QUADS // 2
BODY_SBS = BODY_QUADS // SB_QUADS
BODIES = QUADS // BODY_QUADS
MLP_PARTS = (slice(0, HALF - BODY_PAIRS), slice(HALF - BODY_PAIRS, HALF))
LOAD_SLOTS = 4
HID_SLOTS = 8
WARMUPS = (8, 1)
CANDIDATES_AT = 5
REST_OF_CANDIDATES_AT = 2
DELAY = 9
COPIES = 3
USER_ROWS = 2 * SB_BATCHES

PARAM_COLS = {}
_at = 0
for _name, _width in (("wi", EMB), ("wiT", FEAT), ("wk2", 2 * EMB), ("wq2", 2 * EMB), ("bi", 1), ("wv", 1),
                      ("keep1", 1), ("keep2", 1), ("w1", 3 * HID1), ("w2", HID2), ("w3", HID3), ("wo", 1),
                      ("bo", 1), ("b", 3), ("g", 3), ("be", 3), ("m", 3), ("v", 3)):
    PARAM_COLS[_name] = (_at, _width)
    _at += _width
PARAMS = _at
WK_WQ = slice(PARAM_COLS["wk2"][0] + EMB, PARAM_COLS["wq2"][0] + EMB)
EARLY = PARAM_COLS["w1"][0]


def build(nc, hist_dram, cand_dram, params_dram, lens_dram, out_dram):
    with ExitStack() as ctx:
        def sb(name, shape, dt=F32):
            return ctx.enter_context(nc.sbuf_tensor(name, shape, dt))

        def psum(name, shape):
            return ctx.enter_context(nc.psum_tensor(name, shape, F32))

        def sem(name):
            return ctx.enter_context(nc.semaphore(name))

        params = sb("params", [128, PARAMS])

        def param(name, rows=slice(0, 128)):
            at, width = PARAM_COLS[name]
            return params[rows, at:at + width]

        history = sb("history", [128, LOAD_SLOTS, 2, 4, SEQ])
        candT = sb("candT", [128, USERS])
        warmup = sb("warmup", [128, QCOLS], BF16)
        lens_raw = sb("lens_raw", [128, HALF + SUPERBLOCKS], I32)
        lens = sb("lens", [128, HALF + SUPERBLOCKS])
        pair_len = lens[:, 0:HALF]
        row_len = lens[:, HALF:HALF + SUPERBLOCKS]
        folded = sb("folded", [128, 2 * EMB])
        wv_rows = sb("wv_rows", [128, SB_BATCHES, 32])
        cand = sb("cand", [128, HALF])
        query_bias = sb("query_bias", [128, 1])
        query = sb("query", [128, HALF])
        query_now = sb("query_now", [128, BODY_PAIRS])
        len_now = sb("len_now", [128, BODY_PAIRS])
        rowlen_now = sb("rowlen_now", [128, BODY_SBS])
        item = sb("item", [128, SEQ])
        spread = sb("spread", [128, SB_PAIRS, 2, EMB], BF16)
        hidden = sb("hidden", [128, HID_SLOTS, QCOLS])
        kept = sb("kept", [128, BODY_QUADS, 2, SEQ])
        scratch = sb("scratch", [128, 2, 2, SEQ])
        valid = sb("valid", [128, 2, SEQ], I32)
        scores = sb("scores", [128, 2, SEQ])
        neg_max = sb("neg_max", [128, 1])
        weights = sb("weights", [128, SEQ])
        weight_sum = sb("weight_sum", [128, 1])
        inv_sum = sb("inv_sum", [128, 1])
        part_a = sb("part_a", [128, SEQ], BF16)
        part_b = sb("part_b", [128, SEQ], BF16)
        attn = sb("attn", [128, SEQ])
        rest = sb("rest", [128, SEQ])
        parts = sb("parts", [128, 2, SEQ], BF16)
        sum_now = sb("sum_now", [128, BODY_PAIRS])
        interest_now = sb("interest_now", [128, BODY_PAIRS])
        hist_sum = sb("hist_sum", [128, HALF])
        interest = sb("interest", [128, HALF])
        average = sb("average", [128, HALF])
        inv_len = sb("inv_len", [128, HALF])
        count = sb("count", [128, HALF])
        bn_scale = sb("bn_scale", [128, 3])
        bn_shift = sb("bn_shift", [128, 3])
        bn_power = sb("bn_power", [128, 3])
        x1 = sb("x1", [HID1, 2, HALF])
        x2 = sb("x2", [HID2, 2, HALF])
        x3 = sb("x3", [HID3, 2, HALF])
        table_loader = sb("table_loader", [1, 1])
        result = sb("result", [1, 2, HALF])

        key_ps = psum("key_ps", [128, 2, 512])
        hist_ps = psum("hist_ps", [128, 2, 512])
        score_ps = psum("score_ps", [128, 2, 512])
        attn_ps = psum("attn_ps", [128, 2, 512])
        w1 = param("w1").rearrange("p (c n) -> p c n", c=3)
        z1 = key_ps[:, :, 0:HALF]
        z2, z3, z4 = (score_ps[0:n, bank, :].rearrange("p (h n) -> p h n", h=2)
                      for n, bank in ((HID2, 0), (HID3, 0), (1, 1)))

        def attn_bank(t, r):
            if isinstance(t, int) and t == BODIES and r >= 2:
                return (attn_ps[:, 1, :], attn_ps[:, 0, :], hist_ps[:, 0, :], hist_ps[:, 1, :])[r % 4], 4
            return attn_ps[:, (r - DELAY) % 2, :], 2

        warmup_cleared = sem("warmup_cleared")
        early_landed = sem("early_landed")
        late_landed = sem("late_landed")
        first_cand_landed = sem("first_cand_landed")
        cand_landed = sem("cand_landed")
        lens_landed = sem("lens_landed")
        batch_landed = [sem(f"batch_landed{i}") for i in range(LOAD_SLOTS)]
        first_quad_landed = sem("first_quad_landed")
        item_made = sem("item_made")
        spread_made = sem("spread_made")
        wv_steps = sem("wv_steps")
        wv_ready = sem("wv_ready")
        lens_ready = sem("lens_ready")
        folded_product = sem("folded_product")
        folded_ready = sem("folded_ready")
        bias_product = sem("bias_product")
        bias_ready = sem("bias_ready")
        cand_product = sem("cand_product")
        cand_ready = sem("cand_ready")
        query_product = sem("query_product")
        query_ready = sem("query_ready")
        query_staged = sem("query_staged")
        len_staged = sem("len_staged")
        rowlen_staged = sem("rowlen_staged")
        key_ready = sem("key_ready")
        hist_ready = sem("hist_ready")
        relu_done = sem("relu_done")
        masked_summed = sem("masked_summed")
        scored = sem("scored")
        mask_ready = sem("mask_ready")
        scores_taken = sem("scores_taken")
        max_ready = sem("max_ready")
        exp_done = sem("exp_done")
        inv_ready = sem("inv_ready")
        split_steps = sem("split_steps")
        parts_ready = sem("parts_ready")
        attn_spread = sem("attn_spread")
        attn_summed = sem("attn_summed")
        sums_stored = sem("sums_stored")
        bn_steps = sem("bn_steps")
        bn_ready = sem("bn_ready")
        count_ready = sem("count_ready")
        inv_len_ready = sem("inv_len_ready")
        mean_steps = sem("mean_steps")
        average_ready = sem("average_ready")
        interest_ready = sem("interest_ready")
        z1_ready = sem("z1_ready")
        x1_ready = sem("x1_ready")
        z2_ready = sem("z2_ready")
        x2_ready = sem("x2_ready")
        z3_ready = sem("z3_ready")
        x3_ready = sem("x3_ready")
        z4_ready = sem("z4_ready")
        result_ready = sem("result_ready")
        result_stored = sem("result_stored")

        block = ctx.enter_context(nc.Block())

        def wait(eng, semaphore, value):
            if not isinstance(value, int) or value > 0:
                eng.wait_ge(semaphore, value)

        def wait_apart(eng, *waits):
            waits = [(s, v if isinstance(v, int) else eng.to_reg(v)) for s, v in waits]
            eng.wait_ge(lens_ready, 1)
            for semaphore, value in waits:
                wait(eng, semaphore, value)

        @block.sync
        def _(sp):
            def load(t, batch):
                wait(sp, hist_ready, 2 * (BODY_BATCHES * t + batch - LOAD_SLOTS + 1))
                slot = batch % LOAD_SLOTS
                sp.dma_start(history[:, slot, :, :, :].rearrange("f h p s -> f (h p s)"),
                             hist_dram[bass.ds(BODY_BATCHES * t + batch, 1), :, :].rearrange("a f c -> (a f) c"))\
                  .then_inc(batch_landed[slot], 16)

            hist_quads = hist_dram[0, :, :].rearrange("f (h p s) -> f h p s", h=2, p=4)
            sp.dma_start(params[:, 0:EARLY], params_dram[:, 0:EARLY]).then_inc(early_landed, 16)
            sp.dma_start(history[:, 0, :, 0:2, :], hist_quads[:, :, 0:2, :]).then_inc(first_quad_landed, 16)
            cand_halves = cand_dram.rearrange("f (h p) -> f h p", h=2)
            candidates = candT[:, :].rearrange("f (h p) -> f h p", h=2)
            sp.dma_start(candidates[:, :, 0:BODY_PAIRS], cand_halves[:, :, 0:BODY_PAIRS]).then_inc(first_cand_landed, 16)
            sp.dma_start(history[:, 0, :, 2:4, :], hist_quads[:, :, 2:4, :]).then_inc(batch_landed[0], 16)
            sp.dma_start(lens_raw[:, :], lens_dram).then_inc(lens_landed, 16)
            for batch in range(1, BODY_BATCHES):
                load(0, batch)
                if batch == REST_OF_CANDIDATES_AT:
                    sp.dma_start(candidates[:, :, BODY_PAIRS:HALF], cand_halves[:, :, BODY_PAIRS:HALF]).then_inc(cand_landed, 16)
                if batch == LOAD_SLOTS - 1:
                    sp.dma_start(params[:, EARLY:PARAMS], params_dram[:, EARLY:PARAMS]).then_inc(late_landed, 16)
            with sp.Fori(1, BODIES) as t:
                for batch in range(BODY_BATCHES):
                    load(t, batch)
            sp.wait_ge(result_ready, 2)
            sp.dma_start(out_dram.rearrange("(a n) -> a n", a=1), result[:, :, :].rearrange("a h n -> a (h n)")).then_inc(result_stored, 16)
            sp.wait_ge(result_stored, 16)

        @block.gpsimd
        def _(pool):
            pool.iota(item[:, :], pattern=[[1, SEQ]], base=0, channel_multiplier=0,
                      allow_small_or_imprecise_dtypes=True).then_inc(item_made, 1)
            pool.memset(wv_rows[:, :, :], 0.0).then_inc(wv_steps, 1)
            pool.wait_ge(wv_steps, 1)
            wv_view = wv_rows[:, :, :].rearrange("p k (c u) -> p k c u", u=USER_ROWS)
            for h in range(2):
                v = wv_view[64 * h:64 * h + 64, :, 0:COPIES, :]
                pool.affine_select(out=v, in_=v, compare_op=ALU.not_equal, fill=1.0, base=h,
                                   pattern=[[2, SB_BATCHES], [0, COPIES], [-1, USER_ROWS]],
                                   channel_multiplier=0).then_inc(wv_steps, 1)
            pool.wait_ge(wv_steps, 3)
            pool.wait_ge(early_landed, 16)
            pool.tensor_scalar(wv_rows[:, :, :], wv_rows[:, :, :], param("wv"), None, ALU.mult).then_inc(wv_ready, 1)

            flat = spread[:, :, :, :].rearrange("p (k q) h e -> p k q (h e)", q=4)
            pool.memset(spread[:, :, :, :], 0.0).then_inc(spread_made, 1)
            for copy in range(COPIES):
                for h in range(2):
                    v = flat[:, :, :, EMB * h:EMB * h + EMB]
                    if h == 0:
                        pool.wait_ge(spread_made, 2 * copy + 1)
                    pool.affine_select(out=v, in_=v, compare_op=ALU.not_equal, fill=1.0,
                                       base=-USER_ROWS * copy - h, pattern=[[-2, SB_BATCHES], [-32, 4], [0, EMB]],
                                       channel_multiplier=1).then_inc(spread_made, 1)

            pool.wait_ge(lens_ready, 1)

            def prepare(t, j):
                superblock = BODY_SBS * t + j
                wait_apart(pool, (exp_done, superblock - 1))
                if j == 0:
                    wait(pool, mask_ready, 2 * superblock)
                    pool.tensor_copy(rowlen_now[:, :], row_len[:, bass.ds(superblock, BODY_SBS)]).then_inc(rowlen_staged, 1)
                pool.memset(scores[:, j % 2, :], MASKED).then_inc(mask_ready, 1)
                wait_apart(pool, (rowlen_staged, t + 1))
                pool.tensor_scalar(valid[:, j % 2, :], item[:, :], rowlen_now[:, j:j + 1], None,
                                   ALU.is_lt).then_inc(mask_ready, 1)

            def split(t, j):
                superblock = BODY_SBS * t + j
                done = 4 * superblock
                wait_apart(pool, (inv_ready, superblock + 1), (parts_ready, superblock))
                pool.tensor_scalar(attn[:, :], weights[:, :], inv_sum[:, 0:1], 1.0,
                                   ALU.mult, ALU.mult).then_inc(split_steps, 1)
                pool.tensor_scalar(part_a[:, :], weights[:, :], inv_sum[:, 0:1], param("keep1"),
                                   ALU.mult, ALU.mult).then_inc(split_steps, 1)
                wait(pool, split_steps, done + 2)
                pool.tensor_tensor(rest[:, :], attn[:, :], part_a[:, :], ALU.subtract).then_inc(split_steps, 1)
                wait_apart(pool, (split_steps, done + 3))
                pool.tensor_scalar(part_b[:, :], rest[:, :], param("keep2"), 1.0,
                                   ALU.mult, ALU.mult).then_inc(split_steps, 1)
                wait(pool, split_steps, done + 4)
                wait(pool, attn_spread, SB_QUADS * (superblock - 1))
                pool.tensor_tensor(parts[:, j % 2, :], rest[:, :], part_b[:, :],
                                   ALU.subtract).then_inc(parts_ready, 1)

            def body(t, last=False):
                for j in range(BODY_SBS):
                    if last and j == BODY_SBS - 1:
                        return
                    split(t, j)
                    if j < BODY_SBS - 2:
                        prepare(t, j + 2)
                    elif not last:
                        prepare(t + 1, j + 2 - BODY_SBS)

            prepare(0, 0)
            prepare(0, 1)
            pool.wait_ge(late_landed, 16)
            pool.memset(bn_power[:, :], -0.5).then_inc(bn_steps, 1)
            pool.tensor_scalar(bn_scale[:, :], param("v"), BN_EPS, None, ALU.add).then_inc(bn_steps, 1)
            pool.tensor_tensor(bn_shift[:, :], param("b"), param("m"), ALU.subtract).then_inc(bn_steps, 1)
            pool.wait_ge(bn_steps, 3)
            pool.tensor_tensor(bn_scale[:, :], bn_scale[:, :], bn_power[:, :], ALU.pow).then_inc(bn_steps, 1)
            pool.wait_ge(bn_steps, 4)
            pool.tensor_tensor(bn_scale[:, :], bn_scale[:, :], param("g"), ALU.mult).then_inc(bn_steps, 1)
            pool.wait_ge(bn_steps, 5)
            pool.tensor_tensor(bn_shift[:, :], bn_shift[:, :], bn_scale[:, :], ALU.mult).then_inc(bn_steps, 1)
            pool.wait_ge(bn_steps, 6)
            pool.tensor_tensor(bn_shift[:, :], bn_shift[:, :], param("be"), ALU.add).then_inc(bn_ready, 1)
            body(0)
            with pool.Fori(1, BODIES - 1) as t:
                body(t)
            body(BODIES - 1, True)

        @block.scalar
        def _(act):
            def relu_quad(t, r):
                g = BODY_QUADS * t + r
                wait(act, key_ready, g + 1)
                if r % SB_QUADS == 0:
                    wait(act, scored, (BODY_QUADS * t + r - HID_SLOTS) // SB_QUADS + 1 if isinstance(t, int)
                         else BODY_SBS * t + (r - HID_SLOTS) // SB_QUADS + 1)
                for u in range(2):
                    act.activation(hidden[:, r % HID_SLOTS, u * SEQ:(u + 1) * SEQ],
                                   key_ps[:, r % 2, u * SEQ:(u + 1) * SEQ], ACT.Relu,
                                   bias=query_now[:, 2 * r + u:2 * r + u + 1]).then_inc(relu_done, 1)

            def exponent(s, bank):
                wait(act, max_ready, s + 1)
                wait(act, split_steps, 4 * s)
                act.activation(weights[:, :], scores[:, bank, :], ACT.Exp, bias=neg_max[:, 0:1],
                               accum_out=weight_sum[:, 0:1]).then_inc(exp_done, 1)

            def body(t):
                if not isinstance(t, int):
                    wait(act, relu_done, BODY_PAIRS * t)
                    act.activation(query_now[:, :], query[:, bass.ds(BODY_PAIRS * t, BODY_PAIRS)],
                                   ACT.Copy).then_inc(query_staged, 1)
                    wait(act, query_staged, t)
                for r in range(BODY_QUADS):
                    relu_quad(t, r)
                    if r % SB_QUADS == 1 and (r > 1 or not (isinstance(t, int) and t == 0)):
                        exponent(BODY_SBS * t + r // SB_QUADS - 1, (r // SB_QUADS - 1) % 2)

            def mlp_stage(n, stage):
                pairs = MLP_PARTS[n]
                if stage == 1:
                    act.wait_ge(bn_ready, 1)
                    act.wait_ge(z1_ready, n + 1)
                    act.activation(x1[:, :, pairs], z1[:, :, pairs], ACT.Relu, bias=bn_shift[:, 0:1],
                                   scale=bn_scale[:, 0:1]).then_inc(x1_ready, 1)
                if stage == 2:
                    act.wait_ge(z2_ready, n + 1)
                    act.activation(x2[:, :, pairs], z2[:, :, pairs], ACT.Relu, bias=bn_shift[0:HID2, 1:2],
                                   scale=bn_scale[0:HID2, 1:2]).then_inc(x2_ready, 1)
                if stage == 3:
                    act.wait_ge(z3_ready, n + 1)
                    act.activation(x3[:, :, pairs], z3[:, :, pairs], ACT.Relu, bias=bn_shift[0:HID3, 2:3],
                                   scale=bn_scale[0:HID3, 2:3]).then_inc(x3_ready, 1)
                if stage == 4:
                    act.wait_ge(z4_ready, n + 1)
                    act.activation(result[:, :, pairs], z4[:, :, pairs], ACT.Sigmoid,
                                   bias=param("bo", slice(0, 1))).then_inc(result_ready, 1)

            act.wait_ge(query_ready, 1)
            body(0)
            act.wait_ge(query_ready, 2)
            with act.Fori(1, BODIES) as t:
                body(t)
            exponent(SUPERBLOCKS - 1, 1)
            act.activation(table_loader[:, :], param("bo", slice(0, 1)), ACT.Sigmoid)
            for stage in range(1, 4):
                mlp_stage(0, stage)
            mlp_stage(1, 1)
            mlp_stage(1, 2)
            mlp_stage(0, 4)
            mlp_stage(1, 3)
            mlp_stage(1, 4)

        @block.tensor
        def _(pe):
            def keep_busy():
                pe.matmul(score_ps[:, 1, 0:QCOLS], warmup[:, 0:128], warmup[:, :], start=True, stop=True)

            pe.wait_ge(warmup_cleared, 1)
            for _ in range(WARMUPS[0]):
                keep_busy()

            pe.wait_ge(early_landed, 16)
            pe.matmul(attn_ps[:, 0, 0:2 * EMB], param("wiT", slice(0, EMB)), params[0:EMB, WK_WQ],
                      start=True, stop=True).then_inc(folded_product, 1)
            for _ in range(WARMUPS[1]):
                keep_busy()

            def products_of_candidates(out, weights, pairs):
                for h in range(2):
                    product = pe.matmul(out[64 * h:64 * h + 64, pairs], weights,
                                        candT[:, h * HALF + pairs.start:h * HALF + pairs.stop], start=True, stop=True)
                return product

            def first_queries():
                for name in ("wk2", "wq2"):
                    product = pe.matmul(attn_ps[:, 1, 0:1], param(name, slice(0, EMB)), param("bi", slice(0, EMB)),
                                        start=(name == "wk2"), stop=(name == "wq2"))
                product.then_inc(bias_product, 1)
                pe.wait_ge(first_cand_landed, 16)
                products_of_candidates(score_ps[:, 0, :], folded[:, EMB:2 * EMB],
                                       slice(0, BODY_PAIRS)).then_inc(query_product, 1)

            def candidates():
                pe.wait_ge(cand_landed, 16)
                pe.wait_ge(bias_ready, 1)
                products_of_candidates(attn_ps[:, 0, :], folded[:, EMB:2 * EMB], slice(0, HALF)).then_inc(query_product, 1)
                products_of_candidates(attn_ps[:, 1, :], param("wi"), slice(0, HALF)).then_inc(cand_product, 1)

            def project(t, r):
                g = BODY_QUADS * t + r
                batch, pair = r // 2, 2 * (r % 2)
                slot = batch % LOAD_SLOTS
                if isinstance(t, int) and t == 0 and r == 0:
                    pe.wait_ge(first_quad_landed, 16)
                elif r % 2 == 0 or (isinstance(t, int) and t == 0 and r == 1):
                    wait(pe, batch_landed[slot], 16 * (BODY_BATCHES // LOAD_SLOTS * t + batch // LOAD_SLOTS + 1))
                items = [history[:, slot, h, pair:pair + 2, :].rearrange("f p s -> f (p s)") for h in range(2)]
                wait(pe, relu_done, 2 * (g - 2) + 2)
                pe.matmul(key_ps[0:64, r % 2, 0:QCOLS], folded[:, 0:EMB], items[0], start=True, stop=True)
                pe.matmul(key_ps[64:128, r % 2, 0:QCOLS], folded[:, 0:EMB], items[1], start=True, stop=True).then_inc(key_ready, 1)
                wait(pe, masked_summed, 2 * (g - 2) + 2)
                pe.matmul(hist_ps[0:64, r % 2, 0:QCOLS], param("wi"), items[0], start=True, stop=True)
                pe.matmul(hist_ps[64:128, r % 2, 0:QCOLS], param("wi"), items[1], start=True, stop=True).then_inc(hist_ready, 1)

            def score(t, r):
                first_quad = (r - SB_QUADS) % BODY_QUADS
                bank = first_quad // SB_QUADS % 2
                wait(pe, relu_done, 2 * (BODY_QUADS * t + r))
                wait(pe, scores_taken, BODY_SBS * t + r // SB_QUADS - 2)
                for k in range(SB_BATCHES):
                    for q in range(4):
                        quad = first_quad + 2 * k + q // 2
                        product = pe.matmul(score_ps[32 * q:32 * q + 32, bank, 0:SEQ], wv_rows[:, k, :],
                                            hidden[:, quad % HID_SLOTS, (q % 2) * SEQ:(q % 2 + 1) * SEQ],
                                            start=(k == 0), stop=(k == SB_BATCHES - 1))
                product.then_inc(scored, 1)

            def spread_attn(t, r):
                at = r - DELAY
                quad = at % BODY_QUADS
                if quad % SB_QUADS == 0:
                    wait(pe, parts_ready, BODY_SBS * t + at // SB_QUADS + 1)
                bank, ago = attn_bank(t, r)
                wait(pe, attn_summed, 2 * (BODY_QUADS * t + at - ago) + 2)
                for u in range(2):
                    pair = 2 * (quad % SB_QUADS) + u
                    product = pe.matmul(bank[:, u * SEQ:(u + 1) * SEQ],
                                        spread[:, pair, :, :].rearrange("p h e -> p (h e)"),
                                        parts[:, quad // SB_QUADS % 2, :], start=True, stop=True)
                product.then_inc(attn_spread, 1)

            def mlp_stage(n, stage):
                pairs = MLP_PARTS[n]
                if stage == 0:
                    pe.wait_ge(late_landed, 16)
                    pe.wait_ge(average_ready, n + 1)
                    for c, x in ((1, cand), (2, average)):
                        for h in range(2):
                            rows = slice(64 * h, 64 * h + 64)
                            pe.matmul(z1[:, h, pairs], w1[rows, c, :], x[rows, pairs],
                                      start=(c == 1), stop=False, skip_group_check=True)
                if stage == 1:
                    if n == 0:
                        pe.wait_ge(sums_stored, 2 * BODIES - 2)
                    else:
                        pe.wait_ge(interest_ready, 1)
                    for h in range(2):
                        rows = slice(64 * h, 64 * h + 64)
                        product = pe.matmul(z1[:, h, pairs], w1[rows, 0, :], interest[rows, pairs],
                                            start=False, stop=True, skip_group_check=True)
                    product.then_inc(z1_ready, 1)
                if stage == 2:
                    pe.wait_ge(scores_taken, SUPERBLOCKS - 1)
                    pe.wait_ge(x1_ready, n + 1)
                    pe.matmul(z2[:, :, pairs], param("w2"), x1[:, :, pairs], start=True, stop=True).then_inc(z2_ready, 1)
                if stage == 3:
                    pe.wait_ge(x2_ready, n + 1)
                    pe.matmul(z3[:, :, pairs], param("w3", slice(0, HID2)), x2[:, :, pairs],
                              start=True, stop=True).then_inc(z3_ready, 1)
                if stage == 4:
                    pe.wait_ge(scores_taken, SUPERBLOCKS)
                    pe.wait_ge(x3_ready, n + 1)
                    pe.matmul(z4[:, :, pairs], param("wo", slice(0, HID3)), x3[:, :, pairs],
                              start=True, stop=True).then_inc(z4_ready, 1)

            def body(t):
                for r in range(BODY_QUADS):
                    started = not isinstance(t, int) or BODY_QUADS * t + r >= SB_QUADS
                    first = isinstance(t, int) and t == 0
                    project(t, r)
                    if first and r == 0:
                        first_queries()
                    if first and r == CANDIDATES_AT:
                        candidates()
                    if first and r == SB_QUADS:
                        pe.wait_ge(wv_ready, 1)
                    if first and r == DELAY:
                        pe.wait_ge(query_ready, 2)
                        pe.wait_ge(cand_ready, 1)
                        pe.wait_ge(spread_made, 1 + 2 * COPIES)
                    if r % SB_QUADS == 0 and started:
                        score(t, r)
                    if not isinstance(t, int) or BODY_QUADS * t + r >= DELAY:
                        spread_attn(t, r)

            pe.wait_ge(folded_ready, 1)
            body(0)
            with pe.Fori(1, BODIES - 1) as t:
                body(t)
            body(BODIES - 1)
            score(BODIES, 0)
            spread_attn(BODIES, 0)
            spread_attn(BODIES, 1)
            pe.wait_ge(masked_summed, HALF)
            for r in range(2, SB_QUADS):
                spread_attn(BODIES, r)
            pe.wait_ge(relu_done, HALF)
            mlp_stage(0, 0)
            mlp_stage(0, 1)
            spread_attn(BODIES, SB_QUADS)
            mlp_stage(0, 2)
            for r in range(SB_QUADS + 1, DELAY - 1):
                spread_attn(BODIES, r)
            mlp_stage(0, 3)
            spread_attn(BODIES, DELAY - 1)
            mlp_stage(1, 0)
            mlp_stage(1, 1)
            mlp_stage(1, 2)
            mlp_stage(0, 4)
            mlp_stage(1, 3)
            mlp_stage(1, 4)

        @block.vector
        def _(dve):
            dve.memset(warmup[:, :], 0.0).then_inc(warmup_cleared, 1)
            dve.wait_ge(folded_product, 1)
            dve.tensor_copy(folded[:, :], attn_ps[:, 0, 0:2 * EMB]).then_inc(folded_ready, 1)
            dve.wait_ge(lens_landed, 16)
            dve.tensor_copy(lens[:, :], lens_raw[:, :]).then_inc(lens_ready, 1)
            dve.wait_ge(lens_ready, 1)
            dve.tensor_scalar(count[:, :], pair_len, float(SEQ), 0.0, ALU.min, ALU.max).then_inc(count_ready, 1)
            dve.wait_ge(bias_product, 1)
            dve.tensor_copy(query_bias[:, :], attn_ps[:, 1, 0:1]).then_inc(bias_ready, 1)
            dve.wait_ge(bias_ready, 1)
            dve.wait_ge(query_product, 1)
            dve.tensor_scalar(query_now[:, :], score_ps[:, 0, 0:BODY_PAIRS], query_bias[:, 0:1], None,
                              ALU.add).then_inc(query_ready, 1)
            dve.wait_ge(item_made, 1)

            def masked_sum(t, r):
                wait(dve, hist_ready, BODY_QUADS * t + r + 1)
                for u in range(2):
                    col = 2 * r + u
                    dve.scalar_tensor_tensor(out=kept[:, r, u, :], in0=item[:, :], scalar=len_now[:, col:col + 1],
                                             in1=hist_ps[:, r % 2, u * SEQ:(u + 1) * SEQ], op0=ALU.is_lt, op1=ALU.mult,
                                             accum_out=sum_now[:, col:col + 1]).then_inc(masked_summed, 1)

            def attended_sum(t, r, users=(0, 1)):
                at = r - DELAY
                quad = at % BODY_QUADS
                bank = attn_bank(t, r)[0]
                wait(dve, attn_spread, BODY_QUADS * t + at + 1)
                wait(dve, attn_summed, 2 * (BODY_QUADS * t + at - 1))
                for u in users:
                    col = 2 * quad + u
                    dve.tensor_tensor_reduce(scratch[:, quad % 2, u, :], bank[:, u * SEQ:(u + 1) * SEQ],
                                             kept[:, quad, u, :], 1.0, 0.0, ALU.mult, ALU.add,
                                             interest_now[:, col:col + 1]).then_inc(attn_summed, 1)

            def maximum(s, bank):
                wait_apart(dve, (scored, s + 1), (mask_ready, 2 * (s + 1)))
                dve.copy_predicated(scores[:, bank, :], valid[:, bank, :], score_ps[:, bank, 0:SEQ]).then_inc(scores_taken, 1)
                wait(dve, scores_taken, s + 1)
                dve.reduce_max(neg_max[:, 0:1], scores[:, bank, :], AX_X, negate=True).then_inc(max_ready, 1)

            def invert(s):
                wait(dve, exp_done, s + 1)
                dve.reciprocal(inv_sum[:, 0:1], weight_sum[:, 0:1]).then_inc(inv_ready, 1)

            def store_interest(t, stored):
                wait(dve, attn_summed, BODY_PAIRS * (t + 1))
                dve.tensor_scalar(interest[:, bass.ds(BODY_PAIRS * t, BODY_PAIRS)], interest_now[:, :], param("bi"),
                                  None, ALU.add).then_inc(stored, 1)

            def store_hist_sum(t):
                wait(dve, masked_summed, BODY_PAIRS * (t + 1))
                dve.tensor_copy(hist_sum[:, bass.ds(BODY_PAIRS * t, BODY_PAIRS)], sum_now[:, :]).then_inc(sums_stored, 1)

            def mean(n):
                pairs = MLP_PARTS[n]
                dve.wait_ge(count_ready, 1)
                dve.wait_ge(inv_len_ready, 4)
                dve.wait_ge(sums_stored, 2 * BODIES - 2 + n)
                dve.scalar_tensor_tensor(out=average[:, pairs], in0=count[:, pairs], scalar=param("bi"),
                                         in1=hist_sum[:, pairs], op0=ALU.mult, op1=ALU.add).then_inc(mean_steps, 1)
                dve.wait_ge(mean_steps, 1 + n)
                dve.tensor_tensor(average[:, pairs], average[:, pairs], inv_len[:, pairs],
                                  ALU.mult).then_inc(average_ready, 1)

            def body(t, last=False):
                started = not (isinstance(t, int) and t == 0)
                wait(dve, sums_stored, 2 * t - 1)
                dve.tensor_copy(len_now[:, :], pair_len[:, bass.ds(BODY_PAIRS * t, BODY_PAIRS)]).then_inc(len_staged, 1)
                wait(dve, len_staged, t + 1)
                for r in range(BODY_QUADS):
                    j = r // SB_QUADS - 1
                    if r % SB_QUADS == 1 and (started or j >= 0):
                        maximum(BODY_SBS * t + j, j % 2)
                    if r % SB_QUADS == 2 and (started or j >= 0):
                        invert(BODY_SBS * t + j)
                    masked_sum(t, r)
                    if not started and r == CANDIDATES_AT:
                        dve.wait_ge(query_product, 2)
                        dve.tensor_scalar(query[:, :], attn_ps[:, 0, 0:HALF], query_bias[:, 0:1], None,
                                          ALU.add).then_inc(query_ready, 1)
                        dve.wait_ge(cand_product, 1)
                        dve.wait_ge(early_landed, 16)
                        dve.tensor_scalar(cand[:, :], attn_ps[:, 1, 0:HALF], param("bi"), None,
                                          ALU.add).then_inc(cand_ready, 1)
                    if not started and BODY_QUADS - 5 < r < BODY_QUADS:
                        quarter = slice((BODY_QUADS - 1 - r) * HALF // 4, (BODY_QUADS - r) * HALF // 4)
                        dve.reciprocal(inv_len[:, quarter], pair_len[:, quarter]).then_inc(inv_len_ready, 1)
                    if last and r == DELAY:
                        mean(0)
                    if started and r == DELAY:
                        wait(dve, sums_stored, 2 * t)
                    if started or r >= DELAY:
                        attended_sum(t, r)
                    if started and r == DELAY - 1:
                        store_interest(t - 1, sums_stored)
                if not last:
                    store_hist_sum(t)

            body(0)
            with dve.Fori(1, BODIES - 1) as t:
                body(t)
            body(BODIES - 1, last=True)

            s = SUPERBLOCKS - 1
            maximum(s, 1)
            store_hist_sum(BODIES - 1)
            attended_sum(BODIES, 0)
            invert(s)
            mean(1)
            dve.wait_ge(parts_ready, s)
            dve.wait_ge(inv_ready, s + 1)
            dve.tensor_scalar(attn[:, :], weights[:, :], inv_sum[:, 0:1], None, ALU.mult).then_inc(split_steps, 1)
            dve.tensor_scalar(part_a[:, :], weights[:, :], inv_sum[:, 0:1], param("keep1"),
                              ALU.mult, ALU.mult).then_inc(split_steps, 1)
            attended_sum(BODIES, 1, (0,))
            dve.wait_ge(split_steps, 4 * s + 2)
            dve.tensor_tensor(rest[:, :], attn[:, :], part_a[:, :], ALU.subtract).then_inc(split_steps, 1)
            attended_sum(BODIES, 1, (1,))
            dve.wait_ge(split_steps, 4 * s + 3)
            dve.tensor_scalar(part_b[:, :], rest[:, :], param("keep2"), None, ALU.mult).then_inc(split_steps, 1)
            attended_sum(BODIES, 2, (0,))
            dve.wait_ge(split_steps, 4 * s + 4)
            dve.wait_ge(attn_spread, SB_QUADS * (s - 1))
            dve.tensor_tensor(parts[:, (BODY_SBS - 1) % 2, :], rest[:, :], part_b[:, :],
                              ALU.subtract).then_inc(parts_ready, 1)
            attended_sum(BODIES, 2, (1,))
            for r in range(3, DELAY):
                attended_sum(BODIES, r)
            store_interest(BODIES - 1, interest_ready)


def kernel(**inputs):
    import numpy as np
    import concourse.bacc as bacc
    from concourse.bass_utils import run_bass_kernel_spmd

    take = {name: np.ascontiguousarray(value) for name, value in inputs.items()}
    hist = take["r_history_features"].reshape(2, BATCHES, 4, SEQ, FEAT).transpose(1, 4, 0, 2, 3)
    hist = np.ascontiguousarray(hist).reshape(BATCHES, FEAT, 2 * 4 * SEQ)
    cand = np.ascontiguousarray(take["r_candidate_features"].T)
    length = take["r_history_length"]
    lens = np.zeros((128, HALF + SUPERBLOCKS), length.dtype)
    lens[0:64, 0:HALF] = length[0:HALF]
    lens[64:128, 0:HALF] = length[HALF:USERS]
    rows = length.reshape(2, SUPERBLOCKS, SB_BATCHES, 4).transpose(3, 2, 0, 1).reshape(4, USER_ROWS, SUPERBLOCKS)
    row_view = lens[:, HALF:].reshape(4, 32, SUPERBLOCKS)
    for copy in range(COPIES):
        row_view[:, USER_ROWS * copy:USER_ROWS * (copy + 1)] = rows
    lens[:, HALF:] = row_view.reshape(128, SUPERBLOCKS)
    params = np.zeros((128, PARAMS), np.float32)

    def put(name, value, column=0, halves=1):
        at = PARAM_COLS[name][0] + column
        value = value.reshape(value.shape[0], -1)
        n, width = value.shape
        for h in range(halves):
            params[64 * h:64 * h + n, at:at + width] = value

    put("wi", take["L0_rec_Wi"])
    put("wiT", take["L0_rec_Wi"].T)
    for name, source in (("wk2", "Wk"), ("wq2", "Wq")):
        for copy in range(2):
            put(name, take[f"L0_rec_{source}"], copy * EMB)
    for name, source in (("bi", "bi"), ("wv", "Wv")):
        put(name, take[f"L0_rec_{source}"], halves=2)
    row_copy = np.arange(128) % 32 // USER_ROWS
    put("keep1", (row_copy >= 1).astype(np.float32))
    put("keep2", (row_copy >= 2).astype(np.float32))
    for c in range(3):
        put("w1", take["L0_rec_W1"][EMB * c:EMB * (c + 1)], c * HID1, halves=2)
    put("w2", take["L0_rec_W2"])
    put("w3", take["L0_rec_W3"])
    put("wo", take["L0_rec_Wo"])
    put("bo", take["L0_rec_bo"])
    for layer in range(3):
        for name in ("b", "g", "be", "m", "v"):
            put(name, take[f"L0_rec_{name}{layer + 1}"], layer)

    nc = bacc.Bacc("TRN2", target_bir_lowering=False, num_devices=1)
    arrays = {"history_dram": hist, "candidates_dram": cand, "parameters_dram": params, "lengths_dram": lens}
    aps = [nc.dram_tensor(name, a.shape, mybir.dt.from_np(a.dtype), kind="ExternalInput").ap()
           for name, a in arrays.items()]
    out = nc.dram_tensor("probability", (USERS,), F32, kind="ExternalOutput").ap()
    build(nc, *aps, out)
    return run_bass_kernel_spmd(nc, [arrays], core_ids=[0]).results[0]["probability"]
```
